# Optimizing a Trainium2 kernel written in Bass

```python
import numpy as np
import jax
import jax.numpy as jnp

def _softmax(x, axis=-1):
    return jax.nn.softmax(x, axis=axis)

def _gelu(x):
    return jax.nn.gelu(x, approximate=True)

def _silu(x):
    return jax.nn.silu(x)

def _sigmoid(x):
    return jax.nn.sigmoid(x)

def _layernorm(x, axis=-1, eps=1e-05):
    m = jnp.mean(x, axis=axis, keepdims=True)
    v = jnp.var(x, axis=axis, keepdims=True)
    return (x - m) / jnp.sqrt(v + eps)

def _scatter_add(tgt, idx, src, axis=0):
    return tgt.at[idx].add(src)

def _segment_sum(src, seg, n):
    return jax.ops.segment_sum(src, seg, n)
kernel_name = 'mk_xattn_seq_d1_seqx_r8_f2ce05'

def setup_inputs(seed: int=0):
    np.random.seed(seed)
    _w = jnp.asarray

    def _rec_inputs():
        import jax
        import jax.numpy as jnp
        _rk = jax.random.key(seed)
        x = -0.0002928 + 1 * jax.random.normal(jax.random.fold_in(_rk, 1), (32, 128, 128), jnp.float32)
        _lenS = 128 - jax.random.randint(jax.random.fold_in(_rk, 7), (32,), 0, max(1, 128 // 4) + 1, jnp.int32)
        _lenS2 = 128 - jax.random.randint(jax.random.fold_in(_rk, 8), (32,), 0, max(1, 128 // 4) + 1, jnp.int32)
        _ctx_1024P = jax.random.normal(jax.random.fold_in(_rk, 11), (32, 16, 128), jnp.float32)
        _ctx_1024c = jax.random.dirichlet(jax.random.fold_in(_rk, 511), 0.3 * jnp.ones((16,), jnp.float32), (32, 128))
        _ctx_1024t = jnp.einsum('bsk,bkd->bsd', _ctx_1024c, _ctx_1024P)
        _ctx_1024t = _ctx_1024t * jax.lax.rsqrt(jnp.mean(jnp.square(_ctx_1024t)) + 1e-12) * 0.953939
        ctx_1024 = -1.39393e-06 + 0.999914 * (_ctx_1024t + 0.3 * jax.random.normal(jax.random.fold_in(_rk, 611), (32, 128, 128), jnp.float32))
        return (x, ctx_1024)
    x, ctx_1024 = _rec_inputs()

    def _L0_xattn_setup():
        import jax, jax.numpy as jnp
        import numpy as np
        B, S, SE, D, H, FF, E, K = (2, 256, 256, 128, 16, 512, 8, 2)
        HD = D // H

        def _layernorm(x, g, b):
            m = x.mean(-1, keepdims=True)
            v = ((x - m) ** 2).mean(-1, keepdims=True)
            return (x - m) / jnp.sqrt(v + 1e-05) * g + b

        def _attn(q_in, k_in, v_in, wq, bq, wk, bk, wv, bv, wo, bo, causal):
            Bq, Sq, Dm = q_in.shape
            Sk = k_in.shape[1]
            Q = (q_in @ wq + bq).reshape(Bq, Sq, H, HD)
            Kp = (k_in @ wk + bk).reshape(Bq, Sk, H, HD)
            V = (v_in @ wv + bv).reshape(Bq, Sk, H, HD)
            scores = jnp.einsum('bqhd,bkhd->bhqk', Q, Kp) / jnp.sqrt(jnp.float32(HD))
            if causal:
                mask = jnp.tril(jnp.ones((Sq, Sk), bool))
                scores = jnp.where(mask, scores, -jnp.inf)
            a = jax.nn.softmax(scores, axis=-1)
            o = jnp.einsum('bhqk,bkhd->bqhd', a, V).reshape(Bq, Sq, Dm)
            return o @ wo + bo

        def _moe(x, rw, rb, w1, b1, w2, b2):
            T = x.shape[0] * x.shape[1]
            xf = x.reshape(T, D)
            router_weights = jax.nn.softmax(xf @ rw + rb, axis=-1)
            topw, topi = jax.lax.top_k(router_weights, K)
            topw = jax.nn.softmax(topw, axis=-1)
            combine = jnp.zeros((T, E), xf.dtype).at[jnp.arange(T)[:, None], topi].add(topw)
            h = jax.nn.gelu(jnp.einsum('td,edf->etf', xf, w1) + b1[:, None, :], approximate=False)
            eo = jnp.einsum('etf,efd->etd', h, w2) + b2[:, None, :]
            out = jnp.einsum('etd,te->td', eo, combine)
            return out.reshape(x.shape)
        key = jax.random.key(seed)
        ks = jax.random.split(key, 32)
        w = lambda k, shape: jax.random.normal(k, shape, jnp.float32) * 0.02
        inp = {'x': jax.random.normal(ks[0], (B, S, D), jnp.float32), 'encoder_output': jax.random.normal(ks[1], (B, SE, D), jnp.float32), 'sa_wq': w(ks[2], (D, D)), 'sa_bq': jnp.zeros((D,), jnp.float32), 'sa_wk': w(ks[3], (D, D)), 'sa_bk': jnp.zeros((D,), jnp.float32), 'sa_wv': w(ks[4], (D, D)), 'sa_bv': jnp.zeros((D,), jnp.float32), 'sa_wo': w(ks[5], (D, D)), 'sa_bo': jnp.zeros((D,), jnp.float32), 'ca_wq': w(ks[6], (D, D)), 'ca_bq': jnp.zeros((D,), jnp.float32), 'ca_wk': w(ks[7], (D, D)), 'ca_bk': jnp.zeros((D,), jnp.float32), 'ca_wv': w(ks[8], (D, D)), 'ca_bv': jnp.zeros((D,), jnp.float32), 'ca_wo': w(ks[9], (D, D)), 'ca_bo': jnp.zeros((D,), jnp.float32), 'ln1_g': jnp.ones((D,), jnp.float32), 'ln1_b': jnp.zeros((D,), jnp.float32), 'ln2_g': jnp.ones((D,), jnp.float32), 'ln2_b': jnp.zeros((D,), jnp.float32), 'ln3_g': jnp.ones((D,), jnp.float32), 'ln3_b': jnp.zeros((D,), jnp.float32), 'router_w': w(ks[10], (D, E)), 'router_b': jnp.zeros((E,), jnp.float32), 'e_w1': w(ks[11], (E, D, FF)), 'e_b1': jnp.zeros((E, FF), jnp.float32), 'e_w2': w(ks[12], (E, FF, D)), 'e_b2': jnp.zeros((E, D), jnp.float32)}
        return inp
    _L0_xattn_all = _L0_xattn_setup()
    _L0_xattn_in = {k: v for k, v in _L0_xattn_all.items() if k in ('sa_wq', 'sa_bq', 'sa_wk', 'sa_bk', 'sa_wv', 'sa_bv', 'sa_wo', 'sa_bo', 'ca_wq', 'ca_bq', 'ca_wk', 'ca_bk', 'ca_wv', 'ca_bv', 'ca_wo', 'ca_bo', 'ln1_g', 'ln1_b', 'ln2_g', 'ln2_b', 'ln3_g', 'ln3_b', 'router_w', 'router_b', 'e_w1', 'e_b1', 'e_w2', 'e_b2')}
    del _L0_xattn_all
    return {'x': x, 'ctx_1024': ctx_1024, 'L0_xattn_sa_wq': _L0_xattn_in['sa_wq'], 'L0_xattn_sa_bq': _L0_xattn_in['sa_bq'], 'L0_xattn_sa_wk': _L0_xattn_in['sa_wk'], 'L0_xattn_sa_bk': _L0_xattn_in['sa_bk'], 'L0_xattn_sa_wv': _L0_xattn_in['sa_wv'], 'L0_xattn_sa_bv': _L0_xattn_in['sa_bv'], 'L0_xattn_sa_wo': _L0_xattn_in['sa_wo'], 'L0_xattn_sa_bo': _L0_xattn_in['sa_bo'], 'L0_xattn_ca_wq': _L0_xattn_in['ca_wq'], 'L0_xattn_ca_bq': _L0_xattn_in['ca_bq'], 'L0_xattn_ca_wk': _L0_xattn_in['ca_wk'], 'L0_xattn_ca_bk': _L0_xattn_in['ca_bk'], 'L0_xattn_ca_wv': _L0_xattn_in['ca_wv'], 'L0_xattn_ca_bv': _L0_xattn_in['ca_bv'], 'L0_xattn_ca_wo': _L0_xattn_in['ca_wo'], 'L0_xattn_ca_bo': _L0_xattn_in['ca_bo'], 'L0_xattn_ln1_g': _L0_xattn_in['ln1_g'], 'L0_xattn_ln1_b': _L0_xattn_in['ln1_b'], 'L0_xattn_ln2_g': _L0_xattn_in['ln2_g'], 'L0_xattn_ln2_b': _L0_xattn_in['ln2_b'], 'L0_xattn_ln3_g': _L0_xattn_in['ln3_g'], 'L0_xattn_ln3_b': _L0_xattn_in['ln3_b'], 'L0_xattn_router_w': _L0_xattn_in['router_w'], 'L0_xattn_router_b': _L0_xattn_in['router_b'], 'L0_xattn_e_w1': _L0_xattn_in['e_w1'], 'L0_xattn_e_b1': _L0_xattn_in['e_b1'], 'L0_xattn_e_w2': _L0_xattn_in['e_w2'], 'L0_xattn_e_b2': _L0_xattn_in['e_b2']}

def reference(x, ctx_1024, L0_xattn_sa_wq, L0_xattn_sa_bq, L0_xattn_sa_wk, L0_xattn_sa_bk, L0_xattn_sa_wv, L0_xattn_sa_bv, L0_xattn_sa_wo, L0_xattn_sa_bo, L0_xattn_ca_wq, L0_xattn_ca_bq, L0_xattn_ca_wk, L0_xattn_ca_bk, L0_xattn_ca_wv, L0_xattn_ca_bv, L0_xattn_ca_wo, L0_xattn_ca_bo, L0_xattn_ln1_g, L0_xattn_ln1_b, L0_xattn_ln2_g, L0_xattn_ln2_b, L0_xattn_ln3_g, L0_xattn_ln3_b, L0_xattn_router_w, L0_xattn_router_b, L0_xattn_e_w1, L0_xattn_e_b1, L0_xattn_e_w2, L0_xattn_e_b2):
    import jax
    import jax.numpy as jnp

    def _L0_xattn_ref(x, encoder_output, sa_wq, sa_bq, sa_wk, sa_bk, sa_wv, sa_bv, sa_wo, sa_bo, ca_wq, ca_bq, ca_wk, ca_bk, ca_wv, ca_bv, ca_wo, ca_bo, ln1_g, ln1_b, ln2_g, ln2_b, ln3_g, ln3_b, router_w, router_b, e_w1, e_b1, e_w2, e_b2):
        import jax, jax.numpy as jnp
        import numpy as np
        B, S, SE, D, H, FF, E, K = (2, 256, 256, 128, 16, 512, 8, 2)
        HD = D // H

        def _layernorm(x, g, b):
            m = x.mean(-1, keepdims=True)
            v = ((x - m) ** 2).mean(-1, keepdims=True)
            return (x - m) / jnp.sqrt(v + 1e-05) * g + b

        def _attn(q_in, k_in, v_in, wq, bq, wk, bk, wv, bv, wo, bo, causal):
            Bq, Sq, Dm = q_in.shape
            Sk = k_in.shape[1]
            Q = (q_in @ wq + bq).reshape(Bq, Sq, H, HD)
            Kp = (k_in @ wk + bk).reshape(Bq, Sk, H, HD)
            V = (v_in @ wv + bv).reshape(Bq, Sk, H, HD)
            scores = jnp.einsum('bqhd,bkhd->bhqk', Q, Kp) / jnp.sqrt(jnp.float32(HD))
            if causal:
                mask = jnp.tril(jnp.ones((Sq, Sk), bool))
                scores = jnp.where(mask, scores, -jnp.inf)
            a = jax.nn.softmax(scores, axis=-1)
            o = jnp.einsum('bhqk,bkhd->bqhd', a, V).reshape(Bq, Sq, Dm)
            return o @ wo + bo

        def _moe(x, rw, rb, w1, b1, w2, b2):
            T = x.shape[0] * x.shape[1]
            xf = x.reshape(T, D)
            router_weights = jax.nn.softmax(xf @ rw + rb, axis=-1)
            topw, topi = jax.lax.top_k(router_weights, K)
            topw = jax.nn.softmax(topw, axis=-1)
            combine = jnp.zeros((T, E), xf.dtype).at[jnp.arange(T)[:, None], topi].add(topw)
            h = jax.nn.gelu(jnp.einsum('td,edf->etf', xf, w1) + b1[:, None, :], approximate=False)
            eo = jnp.einsum('etf,efd->etd', h, w2) + b2[:, None, :]
            out = jnp.einsum('etd,te->td', eo, combine)
            return out.reshape(x.shape)
        x = _layernorm(x + _attn(x, x, x, sa_wq, sa_bq, sa_wk, sa_bk, sa_wv, sa_bv, sa_wo, sa_bo, True), ln1_g, ln1_b)
        x = _layernorm(x + _attn(x, encoder_output, encoder_output, ca_wq, ca_bq, ca_wk, ca_bk, ca_wv, ca_bv, ca_wo, ca_bo, False), ln2_g, ln2_b)
        x = _layernorm(x + _moe(x, router_w, router_b, e_w1, e_b1, e_w2, e_b2), ln3_g, ln3_b)
        return x
    x = _L0_xattn_ref(x, ctx_1024, L0_xattn_sa_wq, L0_xattn_sa_bq, L0_xattn_sa_wk, L0_xattn_sa_bk, L0_xattn_sa_wv, L0_xattn_sa_bv, L0_xattn_sa_wo, L0_xattn_sa_bo, L0_xattn_ca_wq, L0_xattn_ca_bq, L0_xattn_ca_wk, L0_xattn_ca_bk, L0_xattn_ca_wv, L0_xattn_ca_bv, L0_xattn_ca_wo, L0_xattn_ca_bo, L0_xattn_ln1_g, L0_xattn_ln1_b, L0_xattn_ln2_g, L0_xattn_ln2_b, L0_xattn_ln3_g, L0_xattn_ln3_b, L0_xattn_router_w, L0_xattn_router_b, L0_xattn_e_w1, L0_xattn_e_b1, L0_xattn_e_w2, L0_xattn_e_b2)
    return x

_drawn_inputs = setup_inputs


def setup_inputs(seed=0):
    import zlib

    import numpy as np

    out = dict(_drawn_inputs(seed))
    spreads = {'L0_xattn_sa_bq': (0.0, 0.8),
     'L0_xattn_sa_bk': (0.0, 2.0),
     'L0_xattn_sa_bv': (0.0, 0.27),
     'L0_xattn_sa_bo': (0.0, 0.1),
     'L0_xattn_ca_bq': (0.0, 2.0),
     'L0_xattn_ca_bk': (0.0, 2.0),
     'L0_xattn_ca_bv': (0.0, 0.313),
     'L0_xattn_ca_bo': (0.0, 0.1),
     'L0_xattn_ln1_g': (1.0, 0.2),
     'L0_xattn_ln1_b': (0.0, 0.1),
     'L0_xattn_ln2_g': (1.0, 0.2),
     'L0_xattn_ln2_b': (0.0, 0.1),
     'L0_xattn_ln3_g': (1.0, 0.2),
     'L0_xattn_ln3_b': (0.0, 0.1),
     'L0_xattn_router_b': (0.0, 0.1),
     'L0_xattn_e_b1': (0.0, 0.516),
     'L0_xattn_e_b2': (0.0, 0.1)}
    factors = {'L0_xattn_sa_wq': 8.0,
     'L0_xattn_sa_wk': 8.0,
     'L0_xattn_sa_wv': 4.585,
     'L0_xattn_ca_wq': 8.0,
     'L0_xattn_ca_wk': 8.0}
    for name, (base, spread) in spreads.items():
        noise = np.random.default_rng([zlib.crc32(name.encode()), seed]).standard_normal(out[name].shape)
        drawn = base * np.exp(spread * noise) if base else spread * noise
        out[name] = jnp.asarray(drawn.astype(out[name].dtype))
    for name, factor in factors.items():
        out[name] = (out[name] * factor).astype(out[name].dtype)
    return out
```

```python
from contextlib import ExitStack

import concourse.bass as bass
from concourse import mybir

F32, F16, BF16 = mybir.dt.float32, mybir.dt.float16, mybir.dt.bfloat16
U32, I32 = mybir.dt.uint32, mybir.dt.int32
ALU, ACT, AX = mybir.AluOpType, mybir.ActivationFunctionType, mybir.AxisListType

B, P, D, H, E, FF = 32, 128, 128, 16, 8, 512
HD = D // H
G = 4
HG = H // G
SCALE = float(HD) ** -0.5
EPS = 1e-5
TOK = B * P
ROW = D + 4
TILES = (2 * TOK + E * (P - 1)) // P + 1
SPARE = TILES - 2 * TOK // P
REGION = TOK + P
FC = FF // P
RING, RUNUP = 8, 5

C_ID, C_HM, C_CM, C_SEL, C_UP, C_ONE = 0, 128, 640, 1152, 1664, 1792
C_I8, C_DST, C_I72, C_P, C_SEL0, NCONST = 1920, 1928, 1930, 2002, 2003, 2004
COLS = ["sa_bq", "sa_bk", "sa_bv", "ca_bq", "ca_bk", "ca_bv", "ln1_g", "ln1_b", "ln2_g", "ln2_b"]
ROWS = ["sa_bo", "ca_bo", "ln1_g", "ln1_b", "ln2_g", "ln2_b", "ln3_g", "ln3_b"]
MATS = ["sa_wq", "sa_wk", "sa_wv", "sa_wo", "ca_wq", "ca_wk", "ca_wv", "ca_wo"]

LO, LOOP = 7, 11
FIRST, LAST = -1, B + 5


class Slot:

    def __init__(self, i, t=None, step=2, n=B):
        self.i, self.t, self.step, self.n = i, t, step, n

    def on(self, lag):
        return 0 <= self.i - lag < self.n

    def par(self, lag):
        return (self.i - lag) % 2

    def value(self, v, per_slot):
        return v if self.t is None else v + self.t * (self.step * per_slot)

    def batch(self, lag):
        return self.value(self.i - lag, 1)


class Turns:

    def __init__(self, *kinds):
        self.kinds = kinds
        self.rate = sum(n for _, _, n in kinds)

    def before(self, s, kind, sub=0):
        n = sum(k for i in range(FIRST, s.i) for _, lag, k in self.kinds if 0 <= i - lag < B)
        for name, lag, k in self.kinds:
            if name == kind:
                return n + sub
            n += k * s.on(lag)

    def total(self):
        return B * self.rate


def wait(eng, sem, s, v, rate):
    if v > 0:
        eng.wait_ge(sem, s.value(v, rate))


def each_slot(eng, body, first=FIRST):
    for i in range(first, LO):
        body(Slot(i))
    with eng.Fori(0, LOOP) as t:
        for u in range(2):
            body(Slot(LO + u, t))
    for i in range(LO + 2 * LOOP, LAST):
        body(Slot(i))


def each_tile(eng, body):
    for i in range(-RUNUP, RING):
        body(Slot(i, None, RING, TILES))
    with eng.Fori(0, TILES // RING - 2) as t:
        for u in range(RING):
            body(Slot(RING + u, t, RING, TILES))
    for i in range(TILES - RING, TILES + 3):
        body(Slot(i, None, RING, TILES))


M0 = Turns(("projS", 0, 1), ("trx", -1, 1), ("trc", 1, 1), ("mtC", 3, 1), ("projC", 2, 1), ("mtS", 0, 1))
M1 = Turns(("woC", 4, 1), ("ztC", 4, 1), ("pre", 5, 1), ("woS", 1, 1), ("ztS", 1, 1), ("log", 4, 1))
S1 = Turns(("C", 3, G), ("S", 0, G))
S2 = Turns(("S", 1, G), ("C", 3, G))
OD = Turns(("S", 1, 1), ("C", 3, 1))
LAG1, LAG2 = {"S": 0, "C": 3}, {"S": 1, "C": 3}
PROJ, END = {"S": 0, "C": 2}, {"S": 1, "C": 4}


def build(nc, x, ctx_in, const, cols, rows, mats, rw, rb, w1, b1, w2, b2, out):
    with ExitStack() as ctx:
        def sb(name, shape, dt=F32):
            return ctx.enter_context(nc.sbuf_tensor(name, shape, dt))

        def sem(name):
            return ctx.enter_context(nc.semaphore(name))

        AB = ("S", "C")
        cst = sb("cst", [P, NCONST])
        ident, hmask = cst[:, C_ID:C_ID + P], cst[:, C_HM:C_HM + HG * P].rearrange("p (h q) -> p h q", h=HG)
        ones = cst[:, C_ONE:C_ONE + P]
        identb, upb, onesb = (sb(n, [P, P], BF16) for n in ("identb", "upb", "onesb"))
        negmask = sb("negmask", [P, HG, P], BF16)
        sel = sb("sel", [P, HG, P], BF16)
        col = sb("col", [P, len(COLS)])
        row = sb("row", [P, len(ROWS), D])
        mat = sb("mat", [P, len(MATS), D])
        wom = {a: sb(f"wom{a}", [P, HG, D]) for a in AB}
        rwt, rbt = sb("rwt", [P, E]), sb("rbt", [P, E])
        radd = {a: sb(f"radd{a}", [P, D]) for a in AB}
        xin = [sb(f"xin{k}", [P, D]) for k in range(2)]
        cin = [sb(f"cin{k}", [P, D]) for k in range(2)]
        xT = [sb(f"xT{k}", [P, P]) for k in range(2)]
        cT = [sb(f"cT{k}", [P, P]) for k in range(2)]
        x1T = [sb(f"x1T{k}", [P, P]) for k in range(2)]
        x2T = [sb(f"x2T{k}", [P, P]) for k in range(2)]

        def two(name, shape, dt=F32):
            return {a: [sb(f"{name}{a}{k}", shape, dt) for k in range(2)] for a in AB}
        qT, kT, v = two("qT", [P, P]), two("kT", [P, P]), two("v", [P, D])
        q16, qm, km = two("q16", [P, P], F16), two("qm", [P, HG, P]), two("km", [P, HG, P], F16)
        nmax, nmaxT = two("nmax", [P, P], BF16), two("nmaxT", [P, P], BF16)
        pT = {a: [sb(f"pT{a}{j}", [P, HG, P]) for j in range(G)] for a in AB}
        rden = sb("rden", [P, HG * P])
        oT = {a: sb(f"oT{a}", [P, HG, P]) for a in AB}
        xb = two("xb", [P, D])
        res, stat, mv = two("res", [P, D]), two("stat", [P, 6]), two("mv", [P, 2])
        ve, rstd, z = two("ve", [P, 1]), two("rstd", [P, 1]), two("z", [P, D])
        zg = {a: sb(f"zg{a}", [P, D]) for a in AB}
        nhalf, carrier, eps = sb("nhalf", [P, 1]), sb("carrier", [P, 1]), sb("eps", [P, 1])

        def ps(name, dt=F32, n=512):
            return ctx.enter_context(nc.psum_tensor(name, [P, n], dt))
        ps1, ps2 = [ps("ps1a"), ps("ps1b")], [ps("ps2a"), ps("ps2b")]
        po, pd, m0, m1 = ps("po"), ps("pd"), ps("m0"), ps("m1")
        m0b = m0[:, 0:P // 2].bitcast(BF16)

        ld_const = sem("ld_const")
        ld_x, ld_c, dbg = ([sem(f"{n}{k}") for k in range(2)] for n in ("ld_x", "ld_c", "dbg"))
        cast_done, zero_done, radd_mm, radd_done = sem("cast_done"), sem("zero_done"), sem("radd_mm"), sem("radd_done")
        m0_written, m0_read, m1_written, m1_read = map(sem, ("m0_written", "m0_read", "m1_written", "m1_read"))
        s1_written, s1_read, s2_written, s2_read = map(sem, ("s1_written", "s1_read", "s2_written", "s2_read"))
        av_done, od_read = sem("av_done"), sem("od_read")
        rden_done = sem("rden_done")
        masked = {a: sem(f"masked{a}") for a in AB}
        evac = {a: sem(f"evac{a}") for a in AB}
        ln_dve = {a: sem(f"ln_dve{a}") for a in AB}
        ln_pool = {a: sem(f"ln_pool{a}") for a in AB}
        wo_done = {a: sem(f"wo_done{a}") for a in AB}
        sel_done = sem("sel_done")
        xb_done = sem("xb_done")

        R = [sb(f"R{k}", [P, 2, ROW]) for k in range(2)]

        def pair(name, shape, dt=F32):
            return [sb(f"{name}{k}", shape, dt) for k in range(2)]
        lg, neg, ex = pair("lg", [P, E]), pair("neg", [P, 1]), pair("ex", [P, E])
        esum, rsum, prob, pmax = pair("esum", [P, 1]), pair("rsum", [P, 1]), pair("prob", [P, E]), pair("pmax", [P, E])
        pidx, pidf, hot = pair("pidx", [P, E], U32), pair("pidf", [P, 2]), pair("hot", [P, 2, E])
        picked, e2, wden = pair("picked", [P, E], BF16), pair("e2", [P, 1]), pair("wden", [P, 1])
        place, hotp, rowf, rown = pair("place", [P, E]), pair("hotp", [P, 2, E]), pair("rowf", [P, 2]), pair("rown", [P, 2], U32)
        ride, ride_pool = sb("ride", [P, 1]), sb("ride_pool", [P, 1])
        base, dstf = sb("base", [P, E]), sb("dstf", [P, 2])
        xs = nc.dram_tensor("xs", (E * REGION + SPARE * P, ROW), F32, kind="Internal").ap()
        ys = nc.dram_tensor("ys", (2 * TOK + (E + SPARE) * P, D), F32, kind="Internal").ap()
        RT = 18
        rt_dve, rt_act = sem("rt_dve"), sem("rt_act")
        scattered = [sem(f"scattered{k}") for k in range(2)]
        rode = sem("rode")
        R_set, base_set = sem("R_set"), sem("base_set")
        NE = E + SPARE
        blank = sb("blank", [P, NE, ROW])
        blank_dst = sb("blank_dst", [P, NE], U32)
        plan_dve, blank_set, padded, spare_set = sem("plan_dve"), sem("blank_set"), sem("padded"), sem("spare_set")
        cnt, cnti, nt, cum, delta = sb("cnt", [P, E]), sb("cnti", [P, E], I32), sb("nt", [P, E]), sb("cum", [P, E]), sb("delta", [P, E])
        padf, padn = sb("padf", [P, E]), sb("padn", [P, E], U32)
        past, pastd = sb("past", [P, TILES, E]), sb("pastd", [P, TILES, E])
        tef, trf = sb("tef", [P, TILES]), sb("trf", [P, TILES])
        tile_e, tile_r = sb("tile_e", [P, TILES], I32), sb("tile_r", [P, TILES], I32)
        w1t, w2t = sb("w1t", [P, E, FF]), sb("w2t", [P, E, FC, D])
        bt = sb("bt", [E, FF + D])
        bpart = [sb(f"bpart{k}", [E, FF + D], BF16) for k in range(3)]
        brest = [sb(f"brest{k}", [E, FF + D]) for k in range(2)]
        bp = sb("bp", [3, E, FF + D], BF16)
        bd = nc.dram_tensor("bd", (3, E, FF + D), BF16, kind="Internal").ap()
        ld_w, ld_b, b_split, b_stored, b_moved = map(sem, ("ld_w", "ld_b", "b_split", "b_stored", "b_moved"))
        xg = [sb(f"xg{k}", [P, ROW]) for k in range(RING)]
        xgT, hS, hT = pair("xgT", [P, P]), pair("hS", [P, FF]), pair("hT", [P, FF])
        xf, ysb = [sb(f"xf{k}", [P, D]) for k in range(RING)], [sb(f"ysb{k}", [P, D]) for k in range(RING)]
        psX, psH, psT, psY = [m0, m1], ps1, ps2, [po, pd]
        xg_in = [sem(f"xg_in{k}") for k in range(RING)]
        y_sent = [sem(f"y_sent{k}") for k in range(RING)]
        x_written, x_read, h_written, h_read = map(sem, ("x_written", "x_read", "h_written", "h_read"))
        ht_written, ht_read, y_written, y_done, xf_done = map(sem, ("ht_written", "ht_read", "y_written", "y_done", "xf_done"))
        NQ = B // 4
        yin, ysum, yz, yg = pair("yin", [P, 4, 2, D]), pair("ysum", [P, 4, D]), pair("yz", [P, 4, D]), pair("yg", [P, 4, D])
        fstat, fmv, fve, frstd = pair("fstat", [P, 4, 6]), pair("fmv", [P, 4, 2]), pair("fve", [P, 4]), pair("frstd", [P, 4])
        y_back, stored = [sem(f"y_back{k}") for k in range(2)], [sem(f"stored{k}") for k in range(2)]
        fin_dve, fin_rstd, fin_g, fin_pool = sem("fin_dve"), sem("fin_rstd"), sem("fin_g"), sem("fin_pool")

        def row4(name):
            return rr[name].rearrange("p (o d) -> p o d", o=1).broadcast_to([P, 4, D])

        def plan_tiles(dve):
            n = [0]

            def step(ins):
                ins.then_inc(plan_dve, 1)
                n[0] += 1
                dve.wait_ge(plan_dve, n[0])

            def over(ap):
                return ap.rearrange("p (o e) -> p o e", o=1).broadcast_to([P, TILES, E])
            step(dve.tensor_tensor(padf[:], base[:], cst[:, C_P:C_P + 1].broadcast_to([P, E]), ALU.add))
            step(dve.tensor_copy(padn[:], padf[:]))
            step(dve.tensor_scalar(cnt[:], cst[:, C_I8:C_I8 + E], -float(REGION), float(P - 1), ALU.mult, ALU.add))
            step(dve.tensor_tensor(cnt[:], cnt[:], base[:], ALU.add))
            step(dve.tensor_copy(cnti[:], cnt[:]))
            step(dve.tensor_scalar(cnti[:], cnti[:], 7, None, ALU.arith_shift_right))
            step(dve.tensor_copy(nt[:], cnti[:]))
            step(dve.tensor_tensor_scan(cum[:], ones[:, 0:E], nt[:], 0.0, ALU.mult, ALU.add))
            step(dve.tensor_scalar(delta[:], nt[:], -float(P), float(REGION), ALU.mult, ALU.add))
            step(dve.tensor_tensor(past[:], cst[:, C_I72:C_I72 + TILES].rearrange("p (i o) -> p i o", o=1)
                                   .broadcast_to([P, TILES, E]), over(cum[:]), ALU.is_ge))
            step(dve.tensor_reduce(tef[:], past[:], AX.X, ALU.add))
            step(dve.tensor_scalar(tile_e[:], tef[:], float(E - 1), None, ALU.min))
            step(dve.tensor_tensor(pastd[:], past[:], over(delta[:]), ALU.mult))
            step(dve.tensor_reduce(trf[:], pastd[:], AX.X, ALU.add))
            step(dve.scalar_tensor_tensor(out=tile_r[:], in0=cst[:, C_I72:C_I72 + TILES], scalar=float(P), in1=trf[:],
                                          op0=ALU.mult, op1=ALU.add))
            assert n[0] == NPLAN

        cb = {n: col[:, k:k + 1] for k, n in enumerate(COLS)}
        rr = {n: row[:, k, :] for k, n in enumerate(ROWS)}
        W = {n: mat[:, k, :] for k, n in enumerate(MATS)}
        pre = {"S": "sa_", "C": "ca_"}
        NLOAD = 6

        block = ctx.enter_context(nc.Block())

        @block.sync
        def _(sp):
            for dst, src in ((cst[:], const), (col[:], cols), (mat[:], mats.rearrange("m p n -> p m n")),
                             (row[:], rows.rearrange("(o r) d -> o r d", o=1).broadcast_to([P, len(ROWS), D])),
                             (rwt[:], rw), (rbt[:], rb.rearrange("(o e) -> o e", o=1).broadcast_to([P, E]))):
                sp.dma_start(dst, src).then_inc(ld_const, 16)
            sp.dma_start(bt[:, 0:FF], b1).then_inc(ld_b, 16)
            sp.dma_start(bt[:, FF:FF + D], b2).then_inc(ld_b, 16)

            def slot(s):
                if s.on(-2):
                    if s.on(0):
                        wait(sp, xb_done, s, s.i + 1, 1)
                    sp.dma_start(xin[s.par(-2)][:],
                                 x[bass.ds(s.batch(-2), 1)].rearrange("o p d -> (o p) d")).then_inc(ld_x[s.par(-2)], 16)
                if s.on(0):
                    if s.on(2):
                        wait(sp, m0_written, s, M0.before(Slot(s.i - 1), "trc") + 1, M0.rate)
                    sp.dma_start(cin[s.par(0)][:],
                                 ctx_in[bass.ds(s.batch(0), 1)].rearrange("o p d -> (o p) d")).then_inc(ld_c[s.par(0)], 16)
            slot(Slot(FIRST - 1))
            slot(Slot(FIRST))
            sp.dma_start(w1t[:], w1.rearrange("e d f -> d e f")).then_inc(ld_w, 16)
            sp.dma_start(w2t[:], w2.rearrange("e (c f) d -> f e c d", f=P)).then_inc(ld_w, 16)
            for k in range(3):
                sp.wait_ge(b_split, 2 * k + 1)
                sp.dma_start(bd[k], bpart[k][:]).then_inc(b_stored, 16)
            sp.wait_ge(b_stored, 48)
            sp.dma_start(bp[:], bd).then_inc(b_moved, 16)
            sp.wait_ge(blank_set, 3)
            for u in range(SPARE):
                sp.dma_start(xs[E * REGION + u * P:E * REGION + (u + 1) * P, :], blank[:, E + u, :]).then_inc(spare_set, 16)
            each_slot(sp, slot, FIRST + 1)
            sp.wait_ge(plan_dve, NPLAN)
            sp.wait_ge(padded, 16 * E)
            sp.wait_ge(spare_set, 16 * SPARE)
            for k in range(2):
                sp.wait_ge(scattered[k], 16 * B)

            def tile_slot(s):
                if s.on(-RUNUP):
                    i = s.i + RUNUP
                    if i >= RING:
                        wait(sp, y_sent[i % RING], s, 16 * (i // RING), 16 // RING)
                    at = i if s.t is None else s.value(i, 1)
                    r = sp.value_load(tile_r[0:1, bass.ds(at, 1)], min_val=0, max_val=E * REGION + SPARE * P - P)
                    sp.dma_start(xg[i % RING][:], xs[bass.ds(r, P), :]).then_inc(xg_in[i % RING], 16)
            each_tile(sp, tile_slot)

            for k in range(RING):
                sp.wait_ge(y_sent[k], 16 * TILES // RING)
            for q in range(NQ + 2):
                k = q % 2
                if q >= 2:
                    sp.wait_ge(fin_pool, 2 * (q - 1))
                    sp.dma_start(out[4 * (q - 2):4 * (q - 1)].rearrange("n p d -> p n d"), yg[k][:]).then_inc(stored[k], 16)
                if q < NQ:
                    sp.dma_start(yin[k][:], ys[8 * P * q:8 * P * (q + 1), :].rearrange("(n p c) d -> p n c d", n=4, c=2))\
                        .then_inc(y_back[k], 16)
            for k in range(2):
                sp.wait_ge(stored[k], 8 * NQ)

        @block.tensor
        def _(pe):
            pe.wait_ge(ld_const, 16 * NLOAD)
            pe.wait_ge(cast_done, NCAST)
            for k, a in enumerate(AB):
                bv = cb[pre[a] + "bv"]
                mm = pe.matmul(m1[:, k * D:k * D + D], bv.broadcast_to([P, P]), W[pre[a] + "wo"],
                               start=True, stop=True)
            mm.then_inc(radd_mm, 1)
            pe.wait_ge(radd_done, 1)

            def max_scores(s, a, j):
                if j == 0:
                    wait(pe, masked[a], s, 3 * (s.i - LAG1[a]) + 3, 3)
                n = S1.before(s, a, j)
                wait(pe, s1_read, s, n - 1, S1.rate)
                k, r = s.par(LAG1[a]), slice(32 * j, 32 * j + 32)
                if a == "S":
                    pe.matmul(ps1[j % 2][:], identb[:], negmask[:], start=True, stop=False)
                pe.matmul(ps1[j % 2][:], q16[a][k][r, :], km[a][k][r, :, :], start=(a == "C"),
                          stop=True).then_inc(s1_written, 1)

            def exp_scores(s, a, j):
                n = S2.before(s, a, j)
                wait(pe, s2_read, s, n - 1, S2.rate)
                if j == 0:
                    wait(pe, m0_read, s, M0.before(s if a == "C" else Slot(s.i - 1), "mt" + a) + 1, M0.rate)
                    wait(pe, masked[a], s, 3 * (s.i - LAG2[a]) + 3, 3)
                k, r = s.par(LAG2[a]), slice(32 * j, 32 * j + 32)
                for h in range(HG):
                    pe.matmul(ps2[j % 2][:, h * P:h * P + P], sel[r, h, :], nmaxT[a][k][r, :],
                              start=(h == 0), stop=False, skip_group_check=True)
                pe.matmul(ps2[j % 2][:], kT[a][k][r, :], qm[a][k][r, :, :], start=False, stop=True,
                          skip_group_check=True).then_inc(s2_written, 1)

            def weigh(s, a, j):
                if j == 0:
                    wait(pe, od_read, s, OD.before(s, a), OD.rate)
                if a == "S":
                    wait(pe, sel_done, s, G * (s.i - 1) + j + 1, G)
                else:
                    wait(pe, s2_read, s, S2.before(s, a, j) + 1, S2.rate)
                r = slice(32 * j, 32 * j + 32)
                pe.matmul(po[r, :], v[a][s.par(LAG2[a])][:, r], pT[a][j][:], start=True, stop=True)
                pe.matmul(pd[r, :], ones[:, 0:32], pT[a][j][:], start=True, stop=True).then_inc(av_done, 1)

            def project(s, a):
                wait(pe, m0_read, s, M0.before(s, "proj" + a), M0.rate)
                k = s.par(PROJ[a])
                if a == "S":
                    src = kv = xT[k][:]
                else:
                    wait(pe, ln_dve["S"], s, 5 * (s.i - 2) + 5, 5)
                    src, kv = x1T[k][:], cT[k][:]
                p = pre[a]
                pe.matmul(m0[:, 0:P], W[p + "wq"], src, start=True, stop=True)
                pe.matmul(m0[:, P:2 * P], W[p + "wk"], kv, start=True, stop=True)
                pe.matmul(m0[:, 2 * P:3 * P], kv, W[p + "wv"], start=True, stop=True).then_inc(m0_written, 1)

            def turn(s, what):
                wait(pe, m0_read, s, M0.before(s, what), M0.rate)
                lag, src, ld = (-1, xin, ld_x) if what == "trx" else (1, cin, ld_c)
                wait(pe, ld[s.par(lag)], s, 16 * ((s.i - lag) // 2 + 1), 8)
                pe.transpose(m0[:, 0:P], src[s.par(lag)][:], ident).then_inc(m0_written, 1)

            def turn_max(s, a):
                wait(pe, m0_read, s, M0.before(s, "mt" + a), M0.rate)
                wait(pe, s1_read, s, S1.before(s, a, G - 1) + 1, S1.rate)
                pe.transpose(m0b, nmax[a][s.par(LAG1[a])][:], identb[:]).then_inc(m0_written, 1)

            def out_proj(s, a):
                wait(pe, m1_read, s, M1.before(s, "wo" + a), M1.rate)
                e = Slot(s.i - 1) if a == "C" else s
                wait(pe, od_read, s, OD.before(e, a) + 1, OD.rate)
                for h in range(HG):
                    mm = pe.matmul(m1[:, 0:D], oT[a][:, h, :], wom[a][:, h, :], start=(h == 0), stop=(h == HG - 1))
                mm.then_inc(m1_written, 1)

            def turn_norm(s, a):
                wait(pe, m1_read, s, M1.before(s, "zt" + a), M1.rate)
                wait(pe, ln_dve[a], s, 5 * (s.i - END[a]) + 4, 5)
                pe.transpose(m1[:, 0:P], z[a][s.par(END[a])][:], ident).then_inc(m1_written, 1)

            def logits(s):
                wait(pe, m1_read, s, M1.before(s, "log"), M1.rate)
                pe.matmul(m1[:, 0:E], x2T[s.par(4)][:], rwt[:], start=True, stop=True).then_inc(m1_written, 1)

            def prefix(s):
                wait(pe, m1_read, s, M1.before(s, "pre"), M1.rate)
                wait(pe, rt_dve, s, RT * (s.i - 5) + 9, RT)
                pe.matmul(m1[:, 0:E], upb[:], picked[s.par(5)][:], start=True, stop=True)
                pe.matmul(m1[:, E:2 * E], onesb[:], picked[s.par(5)][:], start=True, stop=True).then_inc(m1_written, 1)

            def slot(s):
                for j in range(G):
                    if s.on(3):
                        max_scores(s, "C", j)
                    if s.on(1):
                        exp_scores(s, "S", j)
                    if j == 1 and s.on(4):
                        out_proj(s, "C")
                    if j == 2 and s.on(0):
                        project(s, "S")
                    if j and s.on(1):
                        weigh(s, "S", j - 1)
                if s.on(1):
                    weigh(s, "S", G - 1)
                if s.on(4):
                    turn_norm(s, "C")
                if s.on(5):
                    prefix(s)
                if s.on(-1):
                    turn(s, "trx")
                if s.on(1):
                    turn(s, "trc")
                if s.on(3):
                    turn_max(s, "C")
                for j in range(G):
                    if s.on(0):
                        max_scores(s, "S", j)
                    if s.on(3):
                        exp_scores(s, "C", j)
                    if j == 1 and s.on(1):
                        out_proj(s, "S")
                    if j == 2 and s.on(2):
                        project(s, "C")
                    if j and s.on(3):
                        weigh(s, "C", j - 1)
                if s.on(3):
                    weigh(s, "C", G - 1)
                if s.on(1):
                    turn_norm(s, "S")
                if s.on(4):
                    logits(s)
                if s.on(0):
                    turn_max(s, "S")
            each_slot(pe, slot)

            pe.wait_ge(m0_read, M0.total())
            pe.wait_ge(m1_read, M1.total())
            pe.wait_ge(od_read, OD.total())
            pe.wait_ge(s1_read, S1.total())
            pe.wait_ge(s2_read, S2.total())
            pe.wait_ge(plan_dve, NPLAN)
            pe.wait_ge(ld_w, 32)
            pe.wait_ge(b_moved, 16)

            def tile_slot(s):
                i = s.i
                at = i if s.t is None else s.value(i, 1)

                def expert(lag):
                    return pe.value_load(tile_e[0:1, bass.ds(at - lag, 1)], min_val=0, max_val=E - 1)
                if s.on(-1):
                    wait(pe, xg_in[(i + 1) % RING], s, 16 * ((i + 1) // RING + 1), 16 // RING)
                    wait(pe, x_read, s, i, 1)
                    pe.transpose(psX[(i + 1) % 2][:, 0:P], xg[(i + 1) % RING][:, 0:D], ident).then_inc(x_written, 1)
                if s.on(1):
                    wait(pe, h_read, s, i, 1)
                    wait(pe, ht_read, s, i - 2, 1)
                    for c in range(FC):
                        mm = pe.transpose(psT[(i - 1) % 2][:, c * P:c * P + P], hS[(i - 1) % 2][:, c * P:c * P + P], ident)
                    mm.then_inc(ht_written, 1)
                if s.on(0):
                    e = expert(0)
                    wait(pe, x_read, s, i + 1, 1)
                    wait(pe, h_read, s, i - 1, 1)
                    pe.matmul(psH[i % 2][:], onesb[0:3, :], bp[:].rearrange("k e f -> k (e f)")[:, bass.ds(e * (FF + D), FF)],
                              start=True, stop=False)
                    pe.matmul(psH[i % 2][:], xgT[i % 2][:], w1t[:].rearrange("p e f -> p (e f)")[:, bass.ds(e * FF, FF)],
                              start=False, stop=True).then_inc(h_written, 1)
                if s.on(2):
                    e = expert(2)
                    wait(pe, ht_read, s, i - 1, 1)
                    wait(pe, y_done, s, i - 3, 1)
                    pe.matmul(psY[i % 2][:, 0:D], onesb[0:3, :],
                              bp[:].rearrange("k e f -> k (e f)")[:, bass.ds(e * (FF + D) + FF, D)], start=True, stop=False)
                    for c in range(FC):
                        mm = pe.matmul(psY[i % 2][:, 0:D], hT[i % 2][:, c * P:c * P + P],
                                       w2t[:].rearrange("p e c d -> p (e c d)")[:, bass.ds(e * FC * D + c * D, D)],
                                       start=False, stop=(c == FC - 1))
                    mm.then_inc(y_written, 1)
            each_tile(pe, tile_slot)

        @block.scalar
        def _(act):
            def exps(s, a, j):
                n = S2.before(s, a, j)
                wait(act, s2_written, s, n + 1, S2.rate)
                wait(act, av_done, s, n - S2.rate + 1 if s.i - LAG2[a] > 0 else 0, S2.rate)
                act.activation(pT[a][j][:], ps2[j % 2][:].rearrange("p (h q) -> p h q", h=HG), ACT.Exp,
                               scale=SCALE).then_inc(s2_read, 1)

            def copies(s, a):
                n = M0.before(s, "proj" + a)
                wait(act, m0_written, s, n + 1, M0.rate)
                k, p = s.par(PROJ[a]), pre[a]
                if s.i - PROJ[a] >= 2:
                    wait(act, masked[a], s, 3 * (s.i - PROJ[a] - 1), 3)
                    wait(act, av_done, s, S2.before(Slot(s.i - 1 if a == "S" else s.i - 1), a, G - 1) + 1, S2.rate)
                act.activation(kT[a][k][:], m0[:, P:2 * P], ACT.Identity, bias=cb[p + "bk"]).then_inc(evac[a], 1)
                act.activation(qT[a][k][:], m0[:, 0:P], ACT.Identity, bias=cb[p + "bq"]).then_inc(evac[a], 1)
                act.activation(v[a][k][:], m0[:, 2 * P:3 * P], ACT.Copy).then_inc(m0_read, 1)

            def move(s, kind, dst):
                n = M0.before(s, kind)
                wait(act, m0_written, s, n + 1, M0.rate)
                act.activation(dst, m0b if kind[:2] == "mt" else m0[:, 0:P], ACT.Copy).then_inc(m0_read, 1)

            act.wait_ge(ld_const, 16 * NLOAD)

            def router_exp(s):
                k = s.par(5)
                wait(act, rt_dve, s, RT * (s.i - 5) + 2, RT)
                act.activation(ex[k][:], lg[k][:], ACT.Exp, bias=neg[k][:], accum_out=esum[k][:]).then_inc(rt_act, 1)

            def router_two(s):
                k = s.par(5)
                wait(act, rt_dve, s, RT * (s.i - 5) + 5, RT)
                act.activation(e2[k][:], pmax[k][:, 0:1], ACT.Exp, scale=-1.0, bias=pmax[k][:, 1:2]).then_inc(rt_act, 1)

            def slot(s):
                if s.on(5):
                    router_exp(s)
                for j in range(G):
                    if s.on(1):
                        exps(s, "S", j)
                    if j == 2 and s.on(0):
                        copies(s, "S")
                if s.on(5):
                    router_two(s)
                if s.on(-1):
                    move(s, "trx", xT[s.par(-1)][:])
                if s.on(1):
                    move(s, "trc", cT[s.par(1)][:])
                if s.on(3):
                    move(s, "mtC", nmaxT["C"][s.par(3)][:])
                for j in range(G):
                    if s.on(3):
                        exps(s, "C", j)
                    if j == 2 and s.on(2):
                        copies(s, "C")
                if s.on(0):
                    move(s, "mtS", nmaxT["S"][s.par(0)][:])
            each_slot(act, slot)

            def tile_slot(s):
                i = s.i
                if s.on(0):
                    wait(act, h_written, s, i + 1, 1)
                    if i >= 2:
                        wait(act, ht_written, s, i - 1, 1)
                    act.activation(hS[i % 2][:], psH[i % 2][:], ACT.Gelu).then_inc(h_read, 1)
                if s.on(-1):
                    wait(act, x_written, s, i + 2, 1)
                    if i >= 1:
                        wait(act, h_written, s, i, 1)
                    act.activation(xgT[(i + 1) % 2][:], psX[(i + 1) % 2][:, 0:P], ACT.Copy).then_inc(x_read, 1)
            each_tile(act, tile_slot)

        @block.vector
        def _(dve):
            for a in AB:
                for k in range(2):
                    dve.memset(nmax[a][k][:], 0.0).then_inc(zero_done, 1)
            for k in range(2):
                dve.memset(R[k][:, :, D + 3:D + 4], 0.0)
                dve.memset(R[k][:, 0, D + 1:D + 2], 1.0)
                dve.memset(R[k][:, 1, D + 1:D + 2], 0.0).then_inc(R_set, 1)
            dve.wait_ge(ld_const, 16 * NLOAD)
            dve.wait_ge(zero_done, 4)
            dve.tensor_scalar(base[:], cst[:, C_I8:C_I8 + E], float(REGION), None, ALU.mult).then_inc(base_set, 1)
            dve.tensor_copy(dstf[:], cst[:, C_DST:C_DST + 2]).then_inc(base_set, 1)
            dve.wait_ge(base_set, 2)
            dve.wait_ge(ld_b, 32)
            rest = bt
            for k in range(3):
                dve.tensor_copy(bpart[k][:], rest[:]).then_inc(b_split, 1)
                dve.wait_ge(b_split, 2 * k + 1)
                if k < 2:
                    dve.tensor_tensor(brest[k][:], rest[:], bpart[k][:], ALU.subtract).then_inc(b_split, 1)
                    dve.wait_ge(b_split, 2 * k + 2)
                    rest = brest[k]
            dve.wait_ge(radd_mm, 1)
            for k, a in enumerate(AB):
                dve.tensor_tensor(radd[a][:], m1[:, k * D:k * D + D], rr[pre[a] + "bo"], ALU.add).then_inc(radd_done, 1)
            dve.wait_ge(radd_done, 2)
            dve.tensor_tensor(radd["C"][:], radd["C"][:], rr["ln1_b"], ALU.add).then_inc(radd_done, 1)

            def maxima(s, a, j):
                n = S1.before(s, a, j)
                wait(dve, s1_written, s, n + 1, S1.rate)
                if j == 0 and s.i - LAG1[a] >= 2:
                    wait(dve, m0_written, s, M0.before(Slot(s.i - 2), "mt" + a) + 1, M0.rate)
                dve.tensor_reduce(nmax[a][s.par(LAG1[a])][:, 32 * j:32 * j + HG],
                                  ps1[j % 2][:].rearrange("p (h k) -> p h k", h=HG), AX.X, ALU.max,
                                  negate=True).then_inc(s1_read, 1)

            def normalise(s, a):
                n = OD.before(s, a)
                wait(dve, av_done, s, S2.before(s, a, G - 1) + 1, S2.rate)
                dve.reciprocal(rden[:], pd[:]).then_inc(rden_done, 1)
                wait(dve, rden_done, s, n + 1, OD.rate)
                if s.i - LAG2[a] >= 1:
                    wait(dve, m1_written, s, M1.before(Slot(s.i - 1) if a == "S" else s, "wo" + a) + 1, M1.rate)
                dve.tensor_tensor(oT[a][:], po[:].rearrange("p (h q) -> p h q", h=HG),
                                  rden[:].rearrange("p (h q) -> p h q", h=HG), ALU.mult).then_inc(od_read, 1)

            def residual(s, a):
                b, k = s.i - END[a], s.par(END[a])
                wait(dve, m1_written, s, M1.before(s, "wo" + a) + 1, M1.rate)
                if a == "S":
                    wait(dve, xb_done, s, b + 1, 1)
                else:
                    wait(dve, ln_pool["S"], s, 4 * b + 4, 4)
                dve.tensor_tensor(res[a][k][:], m1[:, 0:D], xb[a][k][:], ALU.add).then_inc(m1_read, 1)
                wait(dve, m1_read, s, M1.before(s, "wo" + a) + 1, M1.rate)
                dve.bn_stats(stat[a][k][:], res[a][k][:]).then_inc(ln_dve[a], 1)
                wait(dve, ln_dve[a], s, 5 * b + 1, 5)
                dve.bn_aggr(mv[a][k][:], stat[a][k][:]).then_inc(ln_dve[a], 2)

            def normal(s, a):
                b, k = s.i - END[a], s.par(END[a])
                wait(dve, ln_pool[a], s, (4 if a == "S" else 5) * b + 2, 4 if a == "S" else 5)
                wait(dve, ln_dve[a], s, 5 * b + 3, 5)
                dve.tensor_scalar(z[a][k][:], res[a][k][:], mv[a][k][:, 0:1], rstd[a][k][:],
                                  ALU.subtract, ALU.mult).then_inc(ln_dve[a], 1)

            def affine(s, a):
                k, p = s.par(END[a]), {"S": "ln1_", "C": "ln2_"}[a]
                n = M1.before(s, "zt" + a)
                wait(dve, m1_written, s, n + 1, M1.rate)
                dst = (x1T if a == "S" else x2T)[k]
                dve.tensor_scalar(dst[:], m1[:, 0:P], cb[p + "g"], cb[p + "b"], ALU.mult, ALU.add).then_inc(m1_read, 1)
                wait(dve, m1_read, s, n + 1, M1.rate)
                dve.memset(stat[a][k][:, 0:1], 0.0).then_inc(ln_dve[a], 1)

            def chain(s, lag, n):
                wait(dve, rt_dve, s, RT * (s.i - lag) + n, RT)

            def router_in(s):
                n, k = M1.before(s, "log"), s.par(4)
                wait(dve, m1_written, s, n + 1, M1.rate)
                dve.tensor_tensor(lg[k][:], m1[:, 0:E], rbt[:], ALU.add).then_inc(m1_read, 1)
                wait(dve, m1_read, s, n + 1, M1.rate)
                dve.tensor_reduce(neg[k][:], lg[k][:], AX.X, ALU.max, negate=True).then_inc(rt_dve, 2)

            def router_top(s):
                k = s.par(5)
                wait(dve, rt_act, s, 2 * (s.i - 5) + 1, 2)
                dve.reciprocal(rsum[k][:], esum[k][:]).then_inc(rt_dve, 1)
                chain(s, 5, 3)
                dve.tensor_scalar(prob[k][:], ex[k][:], rsum[k][:], None, ALU.mult).then_inc(rt_dve, 1)
                chain(s, 5, 4)
                dve.tensor_tensor(ride[:], neg[k][:], neg[k][:], ALU.add)
                dve.max(pmax[k][:], prob[k][:]).then_inc(rt_dve, 1)
                chain(s, 5, 5)
                dve.tensor_tensor(ride[:], neg[k][:], neg[k][:], ALU.add)
                dve.max_index(pidx[k][:], pmax[k][:], prob[k][:]).then_inc(rt_dve, 1)
                chain(s, 5, 6)
                dve.tensor_copy(pidf[k][:], pidx[k][:, 0:2]).then_inc(rt_dve, 1)
                chain(s, 5, 7)
                dve.tensor_tensor(hot[k][:], cst[:, C_I8:C_I8 + E].rearrange("p (o e) -> p o e", o=1).broadcast_to([P, 2, E]),
                                  pidf[k][:].rearrange("p (c o) -> p c o", o=1).broadcast_to([P, 2, E]),
                                  ALU.is_equal).then_inc(rt_dve, 1)
                chain(s, 5, 8)
                dve.tensor_tensor(picked[k][:], hot[k][:, 0, :], hot[k][:, 1, :], ALU.add).then_inc(rt_dve, 1)

            def router_out(s):
                n, k, b = M1.before(s, "pre"), s.par(5), s.i - 5
                if b >= 2:
                    wait(dve, scattered[k], s, 32 * (b // 2), 16)
                wait(dve, rt_act, s, 2 * b + 2, 2)
                dve.tensor_scalar(wden[k][:], e2[k][:], 1.0, None, ALU.add).then_inc(rt_dve, 1)
                chain(s, 5, 10)
                dve.reciprocal(R[k][:, 0, D:D + 1], wden[k][:]).then_inc(rt_dve, 1)
                chain(s, 5, 11)
                dve.tensor_tensor(R[k][:, 1, D:D + 1], R[k][:, 0, D:D + 1], e2[k][:], ALU.mult).then_inc(rt_dve, 1)
                dve.tensor_copy(R[k][:, :, D + 2:D + 3].bitcast(U32), dstf[:].rearrange("p (c o) -> p c o", o=1)).then_inc(rt_dve, 1)
                chain(s, 5, 13)
                dve.tensor_scalar(dstf[:], dstf[:], float(2 * P), None, ALU.add).then_inc(rt_dve, 1)
                wait(dve, m1_written, s, n + 1, M1.rate)
                dve.tensor_tensor(place[k][:], m1[:, 0:E], base[:], ALU.add).then_inc(rt_dve, 1)
                chain(s, 5, 15)
                dve.tensor_tensor(base[:], m1[:, E:2 * E], base[:], ALU.add).then_inc(m1_read, 1)
                dve.tensor_tensor(hotp[k][:], hot[k][:], place[k][:].rearrange("p (o e) -> p o e", o=1).broadcast_to([P, 2, E]),
                                  ALU.mult).then_inc(rt_dve, 1)
                chain(s, 5, 16)
                dve.tensor_reduce(rowf[k][:], hotp[k][:], AX.X, ALU.add).then_inc(rt_dve, 1)
                chain(s, 5, 17)
                dve.tensor_copy(rown[k][:], rowf[k][:]).then_inc(rt_dve, 1)
                chain(s, 5, 18)

            def slot(s):
                for j in range(G):
                    if s.on(3):
                        maxima(s, "C", j)
                    if j == 0 and s.on(5):
                        router_top(s)
                    if j == 1 and s.on(4):
                        residual(s, "C")
                    if j == 2 and s.on(4):
                        normal(s, "C")
                if s.on(1):
                    normalise(s, "S")
                if s.on(4):
                    affine(s, "C")
                if s.on(5):
                    router_out(s)
                for j in range(G):
                    if s.on(0):
                        maxima(s, "S", j)
                    if j == 1 and s.on(1):
                        residual(s, "S")
                    if j == 2 and s.on(1):
                        normal(s, "S")
                if s.on(3):
                    normalise(s, "C")
                if s.on(1):
                    affine(s, "S")
                if s.on(4):
                    router_in(s)
            each_slot(dve, slot)
            plan_tiles(dve)

            def tile_slot(s):
                if s.on(1):
                    wait(dve, ht_written, s, s.i, 1)
                    if s.i - 1 >= 2:
                        wait(dve, y_written, s, s.i - 2, 1)
                    dve.tensor_copy(hT[(s.i - 1) % 2][:], psT[(s.i - 1) % 2][:]).then_inc(ht_read, 1)
                if s.on(2):
                    i = s.i - 2
                    wait(dve, y_written, s, i + 1, 1)
                    wait(dve, xf_done, s, i + 1, 1)
                    if i >= RING:
                        wait(dve, y_sent[i % RING], s, 16 * (i // RING), 16 // RING)
                    dve.scalar_tensor_tensor(out=ysb[i % RING][:], in0=psY[i % 2][:, 0:D], scalar=xg[i % RING][:, D:D + 1],
                                             in1=xf[i % RING][:], op0=ALU.mult, op1=ALU.add).then_inc(y_done, 1)
            each_tile(dve, tile_slot)

            for q in range(NQ):
                k = q % 2
                dve.wait_ge(y_back[k], 16 * (q // 2 + 1))
                if q >= 2:
                    dve.wait_ge(fin_pool, 2 * (q - 1))
                dve.tensor_tensor(ysum[k][:], yin[k][:, :, 0, :], yin[k][:, :, 1, :], ALU.add).then_inc(fin_dve, 1)
                dve.wait_ge(fin_dve, 4 * q + 1)
                for c in range(4):
                    ins = dve.bn_stats(fstat[k][:, c, :], ysum[k][:, c, :])
                ins.then_inc(fin_dve, 1)
                dve.wait_ge(fin_dve, 4 * q + 2)
                for c in range(4):
                    ins = dve.bn_aggr(fmv[k][:, c, :], fstat[k][:, c, :])
                ins.then_inc(fin_dve, 1)
                dve.wait_ge(fin_dve, 4 * q + 3)
                dve.wait_ge(fin_rstd, 2 * q + 2)
                for c in range(4):
                    ins = dve.tensor_scalar(yz[k][:, c, :], ysum[k][:, c, :], fmv[k][:, c, 0:1], frstd[k][:, c:c + 1],
                                            ALU.subtract, ALU.mult)
                ins.then_inc(fin_dve, 1)
                dve.wait_ge(fin_dve, 4 * q + 4)
                if q >= 2:
                    dve.wait_ge(stored[k], 16 * (q // 2))
                dve.tensor_tensor(yg[k][:], yz[k][:], row4("ln3_g"), ALU.mult).then_inc(fin_g, 1)

        @block.gpsimd
        def _(pool):
            pool.memset(nhalf[:], -0.5).then_inc(cast_done, 1)
            pool.memset(eps[:], EPS).then_inc(cast_done, 1)
            pool.wait_ge(ld_const, 16 * NLOAD)
            for dst, c, w in ((identb[:], C_ID, P), (upb[:], C_UP, P), (onesb[:], C_ONE, P),
                              (negmask[:].rearrange("p h q -> p (h q)"), C_CM, HG * P),
                              (sel[:].rearrange("p h q -> p (h q)"), C_SEL, HG * P)):
                pool.tensor_copy(dst, cst[:, c:c + w]).then_inc(cast_done, 1)
            for a in AB:
                pool.tensor_tensor(wom[a][:], W[pre[a] + "wo"].rearrange("p (o n) -> p o n", o=1).broadcast_to([P, HG, D]),
                                   hmask, ALU.mult).then_inc(cast_done, 1)
            pool.wait_ge(cast_done, NCAST)
            pool.wait_ge(radd_done, 3)
            pool.memset(blank[:], 0.0).then_inc(blank_set, 1)
            pool.iota(blank_dst[:], pattern=[[P, NE]], base=2 * TOK, channel_multiplier=1).then_inc(blank_set, 1)
            pool.wait_ge(blank_set, 2)
            pool.tensor_copy(blank[:, :, D + 2:D + 3].bitcast(U32), blank_dst[:].rearrange("p (n o) -> p n o", o=1))\
                .then_inc(blank_set, 1)

            def causal(s, j):
                wait(pool, sel_done, s, G * (s.i - 1) + j, G)
                wait(pool, s2_read, s, S2.before(s, "S", j) + 1, S2.rate)
                pool.tensor_tensor(carrier[:], nhalf[:], nhalf[:], ALU.mult)
                pool.affine_select(out=pT["S"][j][:], in_=pT["S"][j][:], compare_op=ALU.is_ge, fill=0.0, base=0,
                                   pattern=[[0, HG], [1, P]], channel_multiplier=-1).then_inc(sel_done, 1)

            def masks(s, a):
                b, k = s.i - PROJ[a], s.par(PROJ[a])
                wait(pool, evac[a], s, 2 * b + 2, 2)
                if b >= 2:
                    wait(pool, s2_written, s, S2.before(Slot(s.i - 1), a, G - 1) + 1, S2.rate)
                pool.tensor_tensor(km[a][k][:], kT[a][k][:].rearrange("p (o n) -> p o n", o=1).broadcast_to([P, HG, P]),
                                   hmask, ALU.mult).then_inc(masked[a], 1)
                pool.tensor_copy(q16[a][k][:], qT[a][k][:]).then_inc(masked[a], 1)
                pool.tensor_tensor(qm[a][k][:], qT[a][k][:].rearrange("p (o n) -> p o n", o=1).broadcast_to([P, HG, P]),
                                   hmask, ALU.mult).then_inc(masked[a], 1)

            def inv_std(s, a):
                b, k, n = s.i - END[a], s.par(END[a]), 4 if a == "S" else 5
                wait(pool, ln_dve[a], s, 5 * b + 3, 5)
                pool.tensor_tensor(ve[a][k][:], mv[a][k][:, 1:2], eps[:], ALU.add).then_inc(ln_pool[a], 1)
                wait(pool, ln_pool[a], s, n * b + 1, n)
                pool.tensor_tensor(rstd[a][k][:], ve[a][k][:], nhalf[:], ALU.pow).then_inc(ln_pool[a], 1)

            def rows_out(s, a):
                b, k, n = s.i - END[a], s.par(END[a]), 4 if a == "S" else 5
                wait(pool, ln_dve[a], s, 5 * b + 4, 5)
                g = rr["ln1_g" if a == "S" else "ln2_g"]
                pool.tensor_tensor(zg[a][:], z[a][k][:], g, ALU.mult).then_inc(ln_pool[a], 1)
                wait(pool, ln_pool[a], s, n * b + 3, n)
                if a == "S":
                    if b >= 2:
                        wait(pool, ln_dve["C"], s, 5 * (b - 2) + 1, 5)
                    pool.tensor_tensor(xb["C"][k][:], zg[a][:], radd["C"][:], ALU.add).then_inc(ln_pool[a], 1)
                else:
                    if b >= 2:
                        wait(pool, scattered[k], s, 32 * (b // 2), 16)
                    for c in range(2):
                        pool.tensor_tensor(R[k][:, c, 0:D], zg[a][:], rr["ln2_b"], ALU.add).then_inc(ln_pool[a], 1)

            def scatter(s):
                k = s.par(5)
                wait(pool, rode, s, s.i - 5, 1)
                wait(pool, ln_pool["C"], s, 5 * (s.i - 5) + 5, 5)
                wait(pool, rt_dve, s, RT * (s.i - 5) + 18, RT)
                pool.tensor_tensor(ride_pool[:], nhalf[:], nhalf[:], ALU.mult).then_inc(rode, 1)
                for c in range(2):
                    pool.indirect_dma_start(out=xs, out_offset=bass.IndirectOffsetOnAxis(ap=rown[k][:, c:c + 1], axis=0),
                                            in_=R[k][:, c, :], in_offset=None).then_inc(scattered[k], 16)

            def slot(s):
                for j in range(G):
                    if s.on(1):
                        causal(s, j)
                    if j == 1 and s.on(4):
                        inv_std(s, "C")
                if s.on(4):
                    rows_out(s, "C")
                if s.on(0):
                    masks(s, "S")
                    wait(pool, m0_written, s, M0.before(Slot(s.i - 1), "trx") + 1, M0.rate)
                    wait(pool, ld_x[s.par(0)], s, 16 * (s.i // 2 + 1), 8)
                    if s.i >= 2:
                        wait(pool, ln_dve["S"], s, 5 * (s.i - 2) + 1, 5)
                    pool.tensor_tensor(xb["S"][s.par(0)][:], xin[s.par(0)][:], radd["S"][:], ALU.add).then_inc(xb_done, 1)
                if s.on(1):
                    inv_std(s, "S")
                if s.on(2):
                    masks(s, "C")
                if s.on(1):
                    rows_out(s, "S")
                if s.on(5):
                    scatter(s)
            each_slot(pool, slot)

            pool.wait_ge(plan_dve, 2)
            for e in range(E):
                pool.indirect_dma_start(out=xs, out_offset=bass.IndirectOffsetOnAxis(ap=padn[:, e:e + 1], axis=0),
                                        in_=blank[:, e, :], in_offset=None).then_inc(padded, 16)

            def tile_slot(s):
                if s.on(2):
                    wait(pool, y_done, s, s.i - 1, 1)
                if s.on(0):
                    i = s.i
                    wait(pool, xg_in[i % RING], s, 16 * (i // RING + 1), 16 // RING)
                    if i >= RING:
                        wait(pool, y_done, s, i - RING + 1, 1)
                    pool.tensor_tensor(xf[i % RING][:], xg[i % RING][:, 0:D], xg[i % RING][:, D + 1:D + 2].broadcast_to([P, D]),
                                       ALU.mult).then_inc(xf_done, 1)
                if s.on(2):
                    i = s.i - 2
                    pool.indirect_dma_start(out=ys, out_offset=bass.IndirectOffsetOnAxis(
                        ap=xg[i % RING][:, D + 2:D + 3].bitcast(U32), axis=0), in_=ysb[i % RING][:, :], in_offset=None)\
                        .then_inc(y_sent[i % RING], 16)
            each_tile(pool, tile_slot)

            for q in range(NQ):
                k = q % 2
                pool.wait_ge(fin_dve, 4 * q + 3)
                pool.tensor_tensor(fve[k][:], fmv[k][:, :, 1], eps[:].broadcast_to([P, 4]), ALU.add).then_inc(fin_rstd, 1)
                pool.wait_ge(fin_rstd, 2 * q + 1)
                pool.tensor_tensor(frstd[k][:], fve[k][:], nhalf[:].broadcast_to([P, 4]), ALU.pow).then_inc(fin_rstd, 1)
                pool.wait_ge(fin_g, q + 1)
                pool.tensor_tensor(yg[k][:], yg[k][:], row4("ln3_b"), ALU.add).then_inc(fin_pool, 2)


NCAST, NPLAN = 9, 15


def constants():
    import numpy as np
    c = np.zeros((P, NCONST), np.float32)
    p = np.arange(P)
    c[:, C_ID:C_ID + P] = np.eye(P)
    for h in range(HG):
        c[:, C_HM + h * P:C_HM + h * P + P] = (p[:, None] // HD % HG == h)
        c[:, C_CM + h * P:C_CM + h * P + P] = np.where(p[None, :] > p[:, None], -1e30, 0.0)
        c[:, C_SEL + h * P:C_SEL + h * P + P] = (p[:, None] % 32 == h)
    c[:, C_UP:C_UP + P] = p[:, None] < p[None, :]
    c[:, C_ONE:C_ONE + P] = 1.0
    c[:, C_I8:C_I8 + E] = np.arange(E)
    c[:, C_DST:C_DST + 2] = 2 * p[:, None] + np.arange(2)
    c[:, C_I72:C_I72 + TILES] = np.arange(TILES)
    c[:, C_P] = p
    c[:, C_SEL0] = 2 * TOK + p
    return c


def kernel(**inputs):
    import numpy as np
    import concourse.bacc as bacc
    from concourse.bass_utils import run_bass_kernel_spmd as run

    def arr(name):
        return np.ascontiguousarray(inputs["L0_xattn_" + name])

    arrays = {
        "x": np.ascontiguousarray(inputs["x"]), "ctx_in": np.ascontiguousarray(inputs["ctx_1024"]),
        "const": constants(), "cols": np.ascontiguousarray(np.stack([arr(n) for n in COLS], 1)),
        "rows": np.stack([arr(n) for n in ROWS]), "mats": np.stack([arr(n) for n in MATS]),
        "rw": arr("router_w"), "rb": arr("router_b"), "w1": arr("e_w1"), "b1": arr("e_b1"),
        "w2": arr("e_w2"), "b2": arr("e_b2"),
    }
    nc = bacc.Bacc("TRN2", target_bir_lowering=False, num_devices=1)
    aps = {n: nc.dram_tensor(n, a.shape, mybir.dt.from_np(a.dtype), kind="ExternalInput").ap() for n, a in arrays.items()}
    out = nc.dram_tensor("out", (B, P, D), F32, kind="ExternalOutput").ap()
    build(nc, out=out, **aps)
    got = run(nc, [arrays], core_ids=[0])
    return got.results[0]["out"]
```

```python
from contextlib import ExitStack

import concourse.bass as bass
from concourse import mybir

F32, F16, BF16 = mybir.dt.float32, mybir.dt.float16, mybir.dt.bfloat16
U32, I32 = mybir.dt.uint32, mybir.dt.int32
ALU, ACT, AX = mybir.AluOpType, mybir.ActivationFunctionType, mybir.AxisListType

B, P, D, H, E, FF = 32, 128, 128, 16, 8, 512
HD = D // H
G = 4
HG = H // G
SPLIT = 3
STACK = 7 * HD
READS = 5
SHIFT = P - 1
SCALE = float(HD) ** -0.5
EPS = 1e-5
TOK = B * P
ROW = D + 4
TILES = (2 * TOK + E * (P - 1)) // P + 1
SPARE = TILES - 2 * TOK // P
REGION = TOK + P
FC = FF // P
RING, RUNUP = 8, 5

C_ID, C_UP, C_ONE, C_CM, C_I8 = 0, P, 2 * P, 3 * P, 7 * P
C_DST, C_I72, C_P, NCONST = C_I8 + E, C_I8 + E + 2, C_I8 + E + 2 + TILES, C_I8 + E + 3 + TILES
COLS = ["sa_bq", "sa_bk", "sa_bv", "ca_bq", "ca_bk", "ca_bv", "ln1_g", "ln1_b", "ln2_g", "ln2_b"]
ROWS = ["sa_bo", "ca_bo", "ln1_g", "ln1_b", "ln2_g", "ln2_b", "ln3_g", "ln3_b"]
MATS = ["sa_wq", "sa_wk", "sa_wv", "sa_wo", "ca_wq", "ca_wk", "ca_wv", "ca_wo"]

LO, LOOP = 11, 9
FIRST, LAST = -1, B + 9


class Slot:

    def __init__(self, i, t=None, step=2, n=B):
        self.i, self.t, self.step, self.n = i, t, step, n

    def on(self, lag):
        return 0 <= self.i - lag < self.n

    def par(self, lag):
        return (self.i - lag) % 2

    def value(self, v, per_slot):
        return v if self.t is None else v + self.t * (self.step * per_slot)

    def batch(self, lag):
        return self.value(self.i - lag, 1)


class Turns:

    def __init__(self, *kinds):
        self.kinds = kinds
        self.rate = sum(n for _, _, n in kinds)

    def before(self, s, kind, sub=0):
        n = sum(k for i in range(FIRST, s.i) for _, lag, k in self.kinds if 0 <= i - lag < B)
        for name, lag, k in self.kinds:
            if name == kind:
                return n + sub
            n += k * s.on(lag)

    def total(self):
        return B * self.rate


def wait(eng, sem, s, v, rate):
    if v > 0:
        eng.wait_ge(sem, s.value(v, rate))


def each_slot(eng, body, first=FIRST):
    for i in range(first, LO):
        body(Slot(i))
    with eng.Fori(0, LOOP) as t:
        for u in range(2):
            body(Slot(LO + u, t))
    for i in range(LO + 2 * LOOP, LAST):
        body(Slot(i))


def each_tile(eng, body):
    for i in range(-RUNUP, RING):
        body(Slot(i, None, RING, TILES))
    with eng.Fori(0, TILES // RING - 2) as t:
        for u in range(RING):
            body(Slot(RING + u, t, RING, TILES))
    for i in range(TILES - RING, TILES + 3):
        body(Slot(i, None, RING, TILES))


MQ = Turns(("projS", 0, 1), ("projC", 4, 1), ("vS", 1, 1), ("vC", 5, 1))
MT = Turns(("mtS", 2, 1), ("otC", 6, 1), ("mtC", 5, 1), ("trx", -1, 1), ("trc", 3, 1), ("otS", 2, 1))
ML = Turns(("woS", 3, 1), ("ztC", 7, 1), ("woC", 6, 1), ("pre", 8, 1), ("ztS", 3, 1), ("log", 7, 1))
S1 = Turns(("C", 5, G), ("S", 1, G))
S2 = Turns(("S", 2, G), ("C", 5, G))
AV = Turns(("C", 6, G), ("S", 2, G))
OD = Turns(("C", 6, 1), ("S", 2, 1))
PROJ, VAL, LAG1, LAG2 = {"S": 0, "C": 4}, {"S": 1, "C": 5}, {"S": 1, "C": 5}, {"S": 2, "C": 5}
WEIGH, END, ROWL = {"S": 2, "C": 6}, {"S": 3, "C": 6}, {"S": 3, "C": 7}
RL, SL = 8, 9


def build(nc, x, ctx_in, const, cols, rows, mats, rw, rb, w1, b1, w2, b2, out):
    with ExitStack() as ctx:
        def sb(name, shape, dt=F32):
            return ctx.enter_context(nc.sbuf_tensor(name, shape, dt))

        def sem(name):
            return ctx.enter_context(nc.semaphore(name))

        AB = ("S", "C")
        cst = sb("cst", [P, NCONST])
        ident = cst[:, C_ID:C_ID + P]
        ones = cst[:, C_ONE:C_ONE + P]
        identb, upb, onesb = (sb(n, [P, P], BF16) for n in ("identb", "upb", "onesb"))
        negmask = sb("negmask", [P, HG, P], BF16)
        col = sb("col", [P, len(COLS)])
        row = sb("row", [P, len(ROWS), D])
        mat = sb("mat", [P, len(MATS), D])
        rwt, rbt = sb("rwt", [P, E]), sb("rbt", [P, E])
        radd = {a: sb(f"radd{a}", [P, D]) for a in AB}
        xin = [sb(f"xin{k}", [P, D]) for k in range(2)]
        cin = [sb(f"cin{k}", [P, D]) for k in range(2)]
        xT = [sb(f"xT{k}", [P, P]) for k in range(2)]
        cT = [sb(f"cT{k}", [P, P]) for k in range(2)]
        x1T = [sb(f"x1T{k}", [P, P]) for k in range(2)]
        x2T = [sb(f"x2T{k}", [P, P]) for k in range(2)]

        def two(name, shape, dt=F32):
            return {a: [sb(f"{name}{a}{k}", shape, dt) for k in range(2)] for a in AB}
        qk = two("qk", [P, 2, P])
        parts, remain = two("parts", [P, 2, SPLIT, P], BF16), two("remain", [P, 2, P])
        stack = {a: [[sb(f"{n}stack{a}{k}", [P, H, P], BF16) for n in "kq"] for k in range(2)] for a in AB}
        v = two("v", [P, H, HD + 1])
        nmax, nmaxT = two("nmax", [P, H], BF16), two("nmaxT", [H, P], BF16)
        pT = {a: [sb(f"pT{a}{j}", [P, HG, P]) for j in range(G)] for a in AB}
        parts_d = {a: [nc.dram_tensor(f"parts_d{a}{k}", (2, SPLIT * HD, H * P), BF16, kind="Internal").ap()
                       for k in range(2)] for a in AB}
        rden = sb("rden", [P, H])
        o, oT = {a: sb(f"o{a}", [P, D]) for a in AB}, {a: sb(f"oT{a}", [P, P]) for a in AB}
        xr = [sb(f"xr{k}", [P, D]) for k in range(2)]
        xb = two("xb", [P, D])
        res, stat, mv = two("res", [P, D]), two("stat", [P, 6]), two("mv", [P, 2])
        ve, rstd, z = two("ve", [P, 1]), two("rstd", [P, 1]), two("z", [P, D])
        zg = two("zg", [P, D])
        part_ride = {a: [sb(f"part_ride{a}{n}", [P, 1]) for n in range(2)] for a in AB}
        nhalf, carrier, eps = sb("nhalf", [P, 1]), sb("carrier", [P, 1]), sb("eps", [P, 1])

        def ps(name, dt=F32, n=512):
            return ctx.enter_context(nc.psum_tensor(name, [P, n], dt))
        ps1, ps2 = [ps("ps1a"), ps("ps1b")], [ps("ps2a"), ps("ps2b")]
        od, mq, mt, ml = ps("od"), ps("mq"), ps("mt"), ps("ml")
        odh = od[:, 0:H * (HD + 1)].rearrange("p (h d) -> p h d", h=H)
        mtb = mt[0:H, 0:P // 2].bitcast(BF16)

        ld_const = sem("ld_const")
        ld_x, ld_c, ld_r = ([sem(f"{n}{k}") for k in range(2)] for n in ("ld_x", "ld_c", "ld_r"))
        cast_done, zero_done, radd_mm, radd_done = sem("cast_done"), sem("zero_done"), sem("radd_mm"), sem("radd_done")
        mq_written, mq_read, mt_written, mt_read = map(sem, ("mq_written", "mq_read", "mt_written", "mt_read"))
        ml_written, ml_read = sem("ml_written"), sem("ml_read")
        s1_written, s1_read, s2_written, s2_read = map(sem, ("s1_written", "s1_read", "s2_written", "s2_read"))
        av_done, od_read = sem("av_done"), sem("od_read")
        rden_done = sem("rden_done")
        cast = {a: sem(f"cast{a}") for a in AB}
        left = {a: sem(f"left{a}") for a in AB}
        parts_out, stack_in, row_in = ({a: [sem(f"{n}{a}{k}") for k in range(2)] for a in AB}
                                       for n in ("parts_out", "stack_in", "row_in"))
        stack_zero, stack_ones = sem("stack_zero"), sem("stack_ones")
        ln_dve = {a: sem(f"ln_dve{a}") for a in AB}
        ln_pool = {a: sem(f"ln_pool{a}") for a in AB}
        row_pool = {a: sem(f"row_pool{a}") for a in AB}
        sel_done = sem("sel_done")
        xb_done = {a: sem(f"xb_done{a}") for a in AB}

        R = [sb(f"R{k}", [P, 2, ROW]) for k in range(2)]

        def pair(name, shape, dt=F32):
            return [sb(f"{name}{k}", shape, dt) for k in range(2)]
        lg, neg, ex = pair("lg", [P, E]), pair("neg", [P, 1]), pair("ex", [P, E])
        esum, rsum, prob, pmax = pair("esum", [P, 1]), pair("rsum", [P, 1]), pair("prob", [P, E]), pair("pmax", [P, E])
        pidx, pidf, hot = pair("pidx", [P, E], U32), pair("pidf", [P, 2]), pair("hot", [P, 2, E])
        picked, e2, wden = pair("picked", [P, E], BF16), pair("e2", [P, 1]), pair("wden", [P, 1])
        place, hotp, rowf, rown = pair("place", [P, E]), pair("hotp", [P, 2, E]), pair("rowf", [P, 2]), pair("rown", [P, 2], U32)
        done = {a: sb(f"done{a}", [P, 1]) for a in AB}
        ride, ride_pool = sb("ride", [P, 1]), sb("ride_pool", [P, 1])
        base, dstf = sb("base", [P, E]), sb("dstf", [P, 2])
        xs = nc.dram_tensor("xs", (E * REGION + SPARE * P, ROW), F32, kind="Internal").ap()
        ys = nc.dram_tensor("ys", (2 * TOK + (E + SPARE) * P, D), F32, kind="Internal").ap()
        RT = 18
        rt_dve, rt_act = sem("rt_dve"), sem("rt_act")
        scattered = [sem(f"scattered{k}") for k in range(2)]
        rode = sem("rode")
        R_set, base_set = sem("R_set"), sem("base_set")
        NE = E + SPARE
        blank = sb("blank", [P, NE, ROW])
        blank_dst = sb("blank_dst", [P, NE], U32)
        plan_dve, blank_set, padded, spare_set = sem("plan_dve"), sem("blank_set"), sem("padded"), sem("spare_set")
        cnt, cnti, nt, cum, delta = sb("cnt", [P, E]), sb("cnti", [P, E], I32), sb("nt", [P, E]), sb("cum", [P, E]), sb("delta", [P, E])
        padf, padn = sb("padf", [P, E]), sb("padn", [P, E], U32)
        past, pastd = sb("past", [P, TILES, E]), sb("pastd", [P, TILES, E])
        tef, trf = sb("tef", [P, TILES]), sb("trf", [P, TILES])
        tile_e, tile_r = sb("tile_e", [P, TILES], I32), sb("tile_r", [P, TILES], I32)
        w1t, w2t = sb("w1t", [P, E, FF]), sb("w2t", [P, E, FC, D])
        bt = sb("bt", [E, FF + D])
        bpart = [sb(f"bpart{k}", [E, FF + D], BF16) for k in range(3)]
        brest = [sb(f"brest{k}", [E, FF + D]) for k in range(2)]
        bp = sb("bp", [3, E, FF + D], BF16)
        bd = nc.dram_tensor("bd", (3, E, FF + D), BF16, kind="Internal").ap()
        ld_w, ld_b, b_split, b_stored, b_moved = map(sem, ("ld_w", "ld_b", "b_split", "b_stored", "b_moved"))
        xg = [sb(f"xg{k}", [P, ROW]) for k in range(RING)]
        xgT, hS, hT = pair("xgT", [P, P]), pair("hS", [P, FF]), pair("hT", [P, FF])
        xf, ysb = [sb(f"xf{k}", [P, D]) for k in range(RING)], [sb(f"ysb{k}", [P, D]) for k in range(RING)]
        psX, psH, psT, psY = [mq, mt], ps1, ps2, [ml, od]
        xg_in = [sem(f"xg_in{k}") for k in range(RING)]
        y_sent = [sem(f"y_sent{k}") for k in range(RING)]
        x_written, x_read, h_written, h_read = map(sem, ("x_written", "x_read", "h_written", "h_read"))
        ht_written, ht_read, y_written, y_done, xf_done = map(sem, ("ht_written", "ht_read", "y_written", "y_done", "xf_done"))
        NQ = B // 4
        yin, ysum, yg = pair("yin", [P, 4, 2, D]), pair("ysum", [P, 4, D]), pair("yg", [P, 4, D])
        fstat, fmv, fve, frstd = pair("fstat", [P, 4, 6]), pair("fmv", [P, 4, 2]), pair("fve", [P, 4]), pair("frstd", [P, 4])
        y_back, stored = [sem(f"y_back{k}") for k in range(2)], [sem(f"stored{k}") for k in range(2)]
        fin_dve, fin_rstd, fin_g, fin_pool = sem("fin_dve"), sem("fin_rstd"), sem("fin_g"), sem("fin_pool")

        def row4(name):
            return rr[name].rearrange("p (o d) -> p o d", o=1).broadcast_to([P, 4, D])

        def plan_tiles(dve):
            n = [0]

            def step(ins):
                ins.then_inc(plan_dve, 1)
                n[0] += 1
                dve.wait_ge(plan_dve, n[0])

            def over(ap):
                return ap.rearrange("p (o e) -> p o e", o=1).broadcast_to([P, TILES, E])
            step(dve.tensor_tensor(padf[:], base[:], cst[:, C_P:C_P + 1].broadcast_to([P, E]), ALU.add))
            step(dve.tensor_copy(padn[:], padf[:]))
            step(dve.tensor_scalar(cnt[:], cst[:, C_I8:C_I8 + E], -float(REGION), float(P - 1), ALU.mult, ALU.add))
            step(dve.tensor_tensor(cnt[:], cnt[:], base[:], ALU.add))
            step(dve.tensor_copy(cnti[:], cnt[:]))
            step(dve.tensor_scalar(cnti[:], cnti[:], 7, None, ALU.arith_shift_right))
            step(dve.tensor_copy(nt[:], cnti[:]))
            step(dve.tensor_tensor_scan(cum[:], ones[:, 0:E], nt[:], 0.0, ALU.mult, ALU.add))
            step(dve.tensor_scalar(delta[:], nt[:], -float(P), float(REGION), ALU.mult, ALU.add))
            step(dve.tensor_tensor(past[:], cst[:, C_I72:C_I72 + TILES].rearrange("p (i o) -> p i o", o=1)
                                   .broadcast_to([P, TILES, E]), over(cum[:]), ALU.is_ge))
            step(dve.tensor_reduce(tef[:], past[:], AX.X, ALU.add))
            step(dve.tensor_scalar(tile_e[:], tef[:], float(E - 1), None, ALU.min))
            step(dve.tensor_tensor(pastd[:], past[:], over(delta[:]), ALU.mult))
            step(dve.tensor_reduce(trf[:], pastd[:], AX.X, ALU.add))
            step(dve.scalar_tensor_tensor(out=tile_r[:], in0=cst[:, C_I72:C_I72 + TILES], scalar=float(P), in1=trf[:],
                                          op0=ALU.mult, op1=ALU.add))
            assert n[0] == NPLAN

        cb = {n: col[:, k:k + 1] for k, n in enumerate(COLS)}
        rr = {n: row[:, k, :] for k, n in enumerate(ROWS)}
        W = {n: mat[:, k, :] for k, n in enumerate(MATS)}
        pre = {"S": "sa_", "C": "ca_"}
        NLOAD = 6

        block = ctx.enter_context(nc.Block())

        @block.sync
        def _(sp):
            for dst, src in ((cst[:], const), (col[:], cols), (mat[:], mats.rearrange("m p n -> p m n")),
                             (row[:], rows.rearrange("(o r) d -> o r d", o=1).broadcast_to([P, len(ROWS), D])),
                             (rwt[:], rw), (rbt[:], rb.rearrange("(o e) -> o e", o=1).broadcast_to([P, E]))):
                sp.dma_start(dst, src).then_inc(ld_const, 16)
            sp.dma_start(bt[:, 0:FF], b1).then_inc(ld_b, 16)
            sp.dma_start(bt[:, FF:FF + D], b2).then_inc(ld_b, 16)

            def shift(s, a):
                k, b = s.par(LAG2[a]), s.i - LAG2[a]
                wait(sp, mt_read, s, MT.before(s, "mt" + a) + 1, MT.rate)
                sp.dma_start(stack[a][k][1][SHIFT:P].rearrange("o h q -> o (h q)"),
                             nmaxT[a][k][:]).then_inc(row_in[a][k], 16)

            def store_parts(s, a):
                k, b = s.par(PROJ[a]), s.i - PROJ[a]
                wait(sp, left[a], s, 2 * b + 2, 2)
                sp.dma_start(parts_d[a][k].rearrange("n (s r) (h t) -> (r h) (n s) t", s=SPLIT, h=H),
                             parts[a][k][:].rearrange("p n s t -> p (n s) t")).then_inc(parts_out[a][k], 16)

            def load_stacks(s, a):
                k, b = s.par(PROJ[a]), s.i - PROJ[a]
                if a == "S" and b >= 2 and not s.on(5):
                    wait(sp, s2_written, s, S2.before(s, a, G - 1) + 1, S2.rate)
                wait(sp, parts_out[a][k], s, 16 * (b // 2 + 1), 8)
                ks, qs = stack[a][k]
                kd, qd = parts_d[a][k][0], parts_d[a][k][1]
                n = SPLIT * HD
                sp.dma_start(ks[0:2 * n],
                             kd.rearrange("(o r) n -> o r n", o=1).broadcast_to([2, n, H * P])).then_inc(stack_in[a][k], 16)
                sp.dma_start(ks[2 * n:STACK], kd[0:HD]).then_inc(stack_in[a][k], 16)
                for u in range(2):
                    sp.dma_start(qs[u * n:u * n + n],
                                 qd[u * HD:u * HD + HD].rearrange("(o r) n -> o r n", o=1)
                                 .broadcast_to([SPLIT, HD, H * P])).then_inc(stack_in[a][k], 16)
                sp.dma_start(qs[2 * n:STACK], qd[2 * HD:n]).then_inc(stack_in[a][k], 16)

            def load(s, lag, src, dst, done):
                sp.dma_start(dst[s.par(lag)][:], src[bass.ds(s.batch(lag), 1)].rearrange("o p d -> (o p) d"))\
                    .then_inc(done[s.par(lag)], 16)

            def slot(s):
                if s.on(2):
                    shift(s, "S")
                if s.on(-2):
                    if s.on(0):
                        wait(sp, mt_written, s, MT.before(Slot(s.i - 1), "trx") + 1, MT.rate)
                    load(s, -2, x, xin, ld_x)
                if s.on(2):
                    if s.i - 2 >= 2:
                        wait(sp, mt_written, s, MT.before(Slot(s.i - 1), "trc") + 1, MT.rate)
                    load(s, 2, ctx_in, cin, ld_c)
                if s.on(1):
                    if s.i - 1 >= 2:
                        wait(sp, xb_done["S"], s, s.i - 2, 1)
                    load(s, 1, x, xr, ld_r)
                if s.on(0):
                    store_parts(s, "S")
                if s.on(4):
                    store_parts(s, "C")
                if s.on(5):
                    shift(s, "C")
                if s.on(4):
                    load_stacks(s, "C")
                if s.on(0):
                    load_stacks(s, "S")
            slot(Slot(FIRST - 1))
            slot(Slot(FIRST))
            sp.wait_ge(stack_zero, 8)
            sp.wait_ge(cast_done, NCAST)
            for a in AB:
                for k in range(2):
                    sp.dma_start(stack[a][k][0][SHIFT:P].rearrange("o h q -> o (h q)"), onesb[0:H, :]).then_inc(stack_ones, 16)
            sp.dma_start(w1t[:], w1.rearrange("e d f -> d e f")).then_inc(ld_w, 16)
            sp.dma_start(w2t[:], w2.rearrange("e (c f) d -> f e c d", f=P)).then_inc(ld_w, 16)
            for k in range(3):
                sp.wait_ge(b_split, 2 * k + 1)
                sp.dma_start(bd[k], bpart[k][:]).then_inc(b_stored, 16)
            sp.wait_ge(b_stored, 48)
            sp.dma_start(bp[:], bd).then_inc(b_moved, 16)
            sp.wait_ge(blank_set, 3)
            for u in range(SPARE):
                sp.dma_start(xs[E * REGION + u * P:E * REGION + (u + 1) * P, :], blank[:, E + u, :]).then_inc(spare_set, 16)
            each_slot(sp, slot, FIRST + 1)
            sp.wait_ge(plan_dve, NPLAN)
            sp.wait_ge(padded, 16 * E)
            sp.wait_ge(spare_set, 16 * SPARE)
            for k in range(2):
                sp.wait_ge(scattered[k], 16 * B)

            def tile_slot(s):
                if s.on(-RUNUP):
                    i = s.i + RUNUP
                    if i >= RING:
                        wait(sp, y_sent[i % RING], s, 16 * (i // RING), 16 // RING)
                    at = i if s.t is None else s.value(i, 1)
                    r = sp.value_load(tile_r[0:1, bass.ds(at, 1)], min_val=0, max_val=E * REGION + SPARE * P - P)
                    sp.dma_start(xg[i % RING][:], xs[bass.ds(r, P), :]).then_inc(xg_in[i % RING], 16)
            each_tile(sp, tile_slot)

            for k in range(RING):
                sp.wait_ge(y_sent[k], 16 * TILES // RING)
            for q in range(NQ + 2):
                k = q % 2
                if q >= 2:
                    sp.wait_ge(fin_pool, 2 * (q - 1))
                    sp.dma_start(out[4 * (q - 2):4 * (q - 1)].rearrange("n p d -> p n d"), yg[k][:]).then_inc(stored[k], 16)
                if q < NQ:
                    sp.dma_start(yin[k][:], ys[8 * P * q:8 * P * (q + 1), :].rearrange("(n p c) d -> p n c d", n=4, c=2))\
                        .then_inc(y_back[k], 16)
            for k in range(2):
                sp.wait_ge(stored[k], 8 * NQ)

        @block.tensor
        def _(pe):
            pe.wait_ge(ld_const, 16 * NLOAD)
            pe.wait_ge(cast_done, NCAST)
            for k, a in enumerate(AB):
                bv = cb[pre[a] + "bv"]
                mm = pe.matmul(ml[:, k * D:k * D + D], bv.broadcast_to([P, P]), W[pre[a] + "wo"],
                               start=True, stop=True)
            mm.then_inc(radd_mm, 1)
            pe.wait_ge(radd_done, 2)
            pe.wait_ge(stack_ones, 64)

            def max_scores(s, a, j):
                k, b = s.par(LAG1[a]), s.i - LAG1[a]
                if j == 0:
                    wait(pe, stack_in[a][k], s, 16 * READS * (b // 2 + 1), 8 * READS)
                wait(pe, s1_read, s, S1.before(s, a, j) - 1, S1.rate)
                ks, qs = stack[a][k]
                for h in range(HG):
                    mm = pe.matmul(ps1[j % 2][:, h * P:h * P + P], qs[0:SHIFT, j * HG + h, :], ks[0:SHIFT, j * HG + h, :],
                                   start=(h == 0 or a == "C"), stop=(a == "C"), skip_group_check=True)
                if a == "S":
                    mm = pe.matmul(ps1[j % 2][:], identb[:], negmask[:], start=False, stop=True, skip_group_check=True)
                mm.then_inc(s1_written, 1)

            def exp_scores(s, a, j):
                k, b = s.par(LAG2[a]), s.i - LAG2[a]
                if j == 0:
                    wait(pe, row_in[a][k], s, 16 * (b // 2 + 1), 8)
                wait(pe, s2_read, s, S2.before(s, a, j) - 1, S2.rate)
                ks, qs = stack[a][k]
                for h in range(HG):
                    mm = pe.matmul(ps2[j % 2][:, h * P:h * P + P], ks[:, j * HG + h, :], qs[:, j * HG + h, :],
                                   start=True, stop=True)
                mm.then_inc(s2_written, 1)

            def weigh(s, a, j):
                b = s.i - WEIGH[a]
                if j == 0:
                    wait(pe, od_read, s, OD.before(s, a), OD.rate)
                    wait(pe, mq_read, s, MQ.before(Slot(s.i - WEIGH[a] + VAL[a]), "v" + a) + 1, MQ.rate)
                if a == "S":
                    wait(pe, sel_done, s, G * b + j + 1, G)
                else:
                    wait(pe, s2_read, s, S2.before(Slot(s.i - WEIGH[a] + LAG2[a]), a, j) + 1, S2.rate)
                for h in range(HG):
                    mm = pe.matmul(odh[:, j * HG + h, :], pT[a][j][:, h, :], v[a][b % 2][:, j * HG + h, :],
                                   start=True, stop=True)
                mm.then_inc(av_done, 1)

            def project(s, a):
                wait(pe, mq_read, s, MQ.before(s, "proj" + a), MQ.rate)
                k = s.par(PROJ[a])
                if a == "S":
                    wait(pe, mt_read, s, MT.before(Slot(s.i - 1), "trx") + 1, MT.rate)
                    src = kv = xT[k][:]
                else:
                    wait(pe, mt_read, s, MT.before(Slot(s.i - 1), "trc") + 1, MT.rate)
                    wait(pe, ln_dve["S"], s, 5 * (s.i - 4) + 5, 5)
                    src, kv = x1T[k][:], cT[k][:]
                p = pre[a]
                pe.matmul(mq[:, 0:P], W[p + "wk"], kv, start=True, stop=True)
                pe.matmul(mq[:, P:2 * P], W[p + "wq"], src, start=True, stop=True).then_inc(mq_written, 1)

            def values(s, a):
                wait(pe, mq_read, s, MQ.before(s, "v" + a), MQ.rate)
                kv = (xT if a == "S" else cT)[s.par(VAL[a])][:]
                pe.matmul(mq[:, 0:D], kv, W[pre[a] + "wv"], start=True, stop=True).then_inc(mq_written, 1)

            def turn(s, what):
                wait(pe, mt_read, s, MT.before(s, what), MT.rate)
                lag, src, ld = (-1, xin, ld_x) if what == "trx" else (3, cin, ld_c)
                wait(pe, ld[s.par(lag)], s, 16 * ((s.i - lag) // 2 + 1), 8)
                pe.transpose(mt[:, 0:P], src[s.par(lag)][:], ident).then_inc(mt_written, 1)

            def turn_max(s, a):
                wait(pe, mt_read, s, MT.before(s, "mt" + a), MT.rate)
                wait(pe, s1_read, s, S1.before(Slot(s.i - LAG2[a] + LAG1[a]), a, G - 1) + 1, S1.rate)
                pe.transpose(mtb, nmax[a][s.par(LAG2[a])][:], identb[:]).then_inc(mt_written, 1)

            def turn_out(s, a):
                wait(pe, mt_read, s, MT.before(s, "ot" + a), MT.rate)
                wait(pe, od_read, s, OD.before(s, a) + 1, OD.rate)
                pe.transpose(mt[:, 0:P], o[a][:], ident).then_inc(mt_written, 1)

            def out_proj(s, a):
                wait(pe, ml_read, s, ML.before(s, "wo" + a), ML.rate)
                wait(pe, mt_read, s, MT.before(Slot(s.i - END[a] + WEIGH[a]), "ot" + a) + 1, MT.rate)
                pe.matmul(ml[:, 0:D], oT[a][:], W[pre[a] + "wo"], start=True, stop=True).then_inc(ml_written, 1)

            def turn_norm(s, a):
                wait(pe, ml_read, s, ML.before(s, "zt" + a), ML.rate)
                wait(pe, ln_dve[a], s, 5 * (s.i - ROWL[a]) + 4, 5)
                pe.transpose(ml[:, 0:P], z[a][s.par(ROWL[a])][:], ident).then_inc(ml_written, 1)

            def logits(s):
                wait(pe, ml_read, s, ML.before(s, "log"), ML.rate)
                pe.matmul(ml[:, 0:E], x2T[s.par(7)][:], rwt[:], start=True, stop=True).then_inc(ml_written, 1)

            def prefix(s):
                wait(pe, ml_read, s, ML.before(s, "pre"), ML.rate)
                wait(pe, rt_dve, s, RT * (s.i - RL) + 9, RT)
                pe.matmul(ml[:, 0:E], upb[:], picked[s.par(RL)][:], start=True, stop=True)
                pe.matmul(ml[:, E:2 * E], onesb[:], picked[s.par(RL)][:], start=True, stop=True).then_inc(ml_written, 1)

            def slot(s):
                def run(lag, f, *args):
                    if s.on(lag):
                        f(s, *args)
                run(6, weigh, "C", 0)
                run(6, weigh, "C", 1)
                run(2, turn_max, "S")
                run(6, weigh, "C", 2)
                run(6, weigh, "C", 3)
                run(0, project, "S")
                run(5, max_scores, "C", 0)
                run(5, max_scores, "C", 1)
                run(4, project, "C")
                run(2, exp_scores, "S", 0)
                run(5, max_scores, "C", 2)
                run(2, exp_scores, "S", 1)
                run(6, turn_out, "C")
                run(5, max_scores, "C", 3)
                run(1, values, "S")
                run(2, exp_scores, "S", 2)
                run(5, values, "C")
                run(2, exp_scores, "S", 3)
                run(3, out_proj, "S")
                run(7, turn_norm, "C")
                run(2, weigh, "S", 0)
                run(5, turn_max, "C")
                run(2, weigh, "S", 1)
                run(2, weigh, "S", 2)
                run(6, out_proj, "C")
                run(2, weigh, "S", 3)
                run(1, max_scores, "S", 0)
                run(1, max_scores, "S", 1)
                run(5, exp_scores, "C", 0)
                run(1, max_scores, "S", 2)
                run(5, exp_scores, "C", 1)
                run(-1, turn, "trx")
                run(1, max_scores, "S", 3)
                run(8, prefix)
                run(5, exp_scores, "C", 2)
                run(3, turn, "trc")
                run(3, turn_norm, "S")
                run(5, exp_scores, "C", 3)
                run(2, turn_out, "S")
                run(7, logits)
            each_slot(pe, slot)

            pe.wait_ge(mq_read, MQ.total())
            pe.wait_ge(mt_read, MT.total())
            pe.wait_ge(ml_read, ML.total())
            pe.wait_ge(od_read, OD.total())
            pe.wait_ge(s1_read, S1.total())
            pe.wait_ge(s2_read, S2.total())
            pe.wait_ge(plan_dve, NPLAN)
            pe.wait_ge(ld_w, 32)
            pe.wait_ge(b_moved, 16)

            def tile_slot(s):
                i = s.i
                at = i if s.t is None else s.value(i, 1)

                def expert(lag):
                    return pe.value_load(tile_e[0:1, bass.ds(at - lag, 1)], min_val=0, max_val=E - 1)
                if s.on(-1):
                    wait(pe, xg_in[(i + 1) % RING], s, 16 * ((i + 1) // RING + 1), 16 // RING)
                    wait(pe, x_read, s, i, 1)
                    pe.transpose(psX[(i + 1) % 2][:, 0:P], xg[(i + 1) % RING][:, 0:D], ident).then_inc(x_written, 1)
                if s.on(1):
                    wait(pe, h_read, s, i, 1)
                    wait(pe, ht_read, s, i - 2, 1)
                    for c in range(FC):
                        mm = pe.transpose(psT[(i - 1) % 2][:, c * P:c * P + P], hS[(i - 1) % 2][:, c * P:c * P + P], ident)
                    mm.then_inc(ht_written, 1)
                if s.on(0):
                    e = expert(0)
                    wait(pe, x_read, s, i + 1, 1)
                    wait(pe, h_read, s, i - 1, 1)
                    pe.matmul(psH[i % 2][:], onesb[0:3, :], bp[:].rearrange("k e f -> k (e f)")[:, bass.ds(e * (FF + D), FF)],
                              start=True, stop=False)
                    pe.matmul(psH[i % 2][:], xgT[i % 2][:], w1t[:].rearrange("p e f -> p (e f)")[:, bass.ds(e * FF, FF)],
                              start=False, stop=True).then_inc(h_written, 1)
                if s.on(2):
                    e = expert(2)
                    wait(pe, ht_read, s, i - 1, 1)
                    wait(pe, y_done, s, i - 3, 1)
                    pe.matmul(psY[i % 2][:, 0:D], onesb[0:3, :],
                              bp[:].rearrange("k e f -> k (e f)")[:, bass.ds(e * (FF + D) + FF, D)], start=True, stop=False)
                    for c in range(FC):
                        mm = pe.matmul(psY[i % 2][:, 0:D], hT[i % 2][:, c * P:c * P + P],
                                       w2t[:].rearrange("p e c d -> p (e c d)")[:, bass.ds(e * FC * D + c * D, D)],
                                       start=False, stop=(c == FC - 1))
                    mm.then_inc(y_written, 1)
            each_tile(pe, tile_slot)

        @block.scalar
        def _(act):
            def exps(s, a, j):
                wait(act, s2_written, s, S2.before(s, a, j) + 1, S2.rate)
                if s.i - LAG2[a] > 0:
                    wait(act, av_done, s, AV.before(Slot(s.i - 1 - LAG2[a] + WEIGH[a]), a, j) + 1, AV.rate)
                act.activation(pT[a][j][:], ps2[j % 2][:].rearrange("p (h q) -> p h q", h=HG), ACT.Exp,
                               scale=SCALE).then_inc(s2_read, 1)

            def projected(s, a):
                k, b, p = s.par(PROJ[a]), s.i - PROJ[a], pre[a]
                wait(act, mq_written, s, MQ.before(s, "proj" + a) + 1, MQ.rate)
                if b >= 2:
                    wait(act, left[a], s, 2 * b - 2, 2)
                act.activation(qk[a][k][:, 0, :], mq[:, 0:P], ACT.Identity, bias=cb[p + "bk"])
                act.activation(qk[a][k][:, 1, :], mq[:, P:2 * P], ACT.Identity, bias=cb[p + "bq"]).then_inc(mq_read, 1)

            def valued(s, a):
                wait(act, mq_written, s, MQ.before(s, "v" + a) + 1, MQ.rate)
                k, b = s.par(VAL[a]), s.i - VAL[a]
                if b >= 2:
                    wait(act, av_done, s, AV.before(Slot(s.i - 2 - VAL[a] + WEIGH[a]), a, G - 1) + 1, AV.rate)
                act.activation(v[a][k][:, :, 0:HD], mq[:, 0:D].rearrange("p (h d) -> p h d", h=H), ACT.Copy)\
                    .then_inc(mq_read, 1)

            def move(s, kind, dst):
                wait(act, mt_written, s, MT.before(s, kind) + 1, MT.rate)
                if kind[:2] == "mt":
                    b = s.i - LAG2[kind[2]]
                    if b >= 2:
                        wait(act, row_in[kind[2]][b % 2], s, 16 * (b // 2), 8)
                if kind[:2] == "ot" and s.i - WEIGH[kind[2]] >= 1:
                    a = kind[2]
                    wait(act, ml_written, s, ML.before(Slot(s.i - 1 - WEIGH[a] + END[a]), "wo" + a) + 1, ML.rate)
                act.activation(dst, mtb if kind[:2] == "mt" else mt[:, 0:P], ACT.Copy).then_inc(mt_read, 1)

            act.wait_ge(ld_const, 16 * NLOAD)
            act.wait_ge(zero_done, 4)

            def router_exp(s):
                k = s.par(RL)
                wait(act, rt_dve, s, RT * (s.i - RL) + 2, RT)
                act.activation(ex[k][:], lg[k][:], ACT.Exp, bias=neg[k][:], accum_out=esum[k][:]).then_inc(rt_act, 1)

            def router_two(s):
                k = s.par(RL)
                wait(act, rt_dve, s, RT * (s.i - RL) + 5, RT)
                act.activation(e2[k][:], pmax[k][:, 0:1], ACT.Exp, scale=-1.0, bias=pmax[k][:, 1:2]).then_inc(rt_act, 1)

            def slot(s):
                def run(lag, f, *args):
                    if s.on(lag):
                        f(s, *args)
                run(2, move, "mtS", nmaxT["S"][s.par(2)][:])
                run(0, projected, "S")
                run(4, projected, "C")
                run(8, router_exp)
                run(2, exps, "S", 0)
                run(2, exps, "S", 1)
                run(6, move, "otC", oT["C"][:])
                run(1, valued, "S")
                run(2, exps, "S", 2)
                run(5, valued, "C")
                run(2, exps, "S", 3)
                run(5, move, "mtC", nmaxT["C"][s.par(5)][:])
                run(8, router_two)
                run(5, exps, "C", 0)
                run(5, exps, "C", 1)
                run(-1, move, "trx", xT[s.par(-1)][:])
                run(5, exps, "C", 2)
                run(3, move, "trc", cT[s.par(3)][:])
                run(5, exps, "C", 3)
                run(2, move, "otS", oT["S"][:])
            each_slot(act, slot)

            def tile_slot(s):
                i = s.i
                if s.on(0):
                    wait(act, h_written, s, i + 1, 1)
                    if i >= 2:
                        wait(act, ht_written, s, i - 1, 1)
                    act.activation(hS[i % 2][:], psH[i % 2][:], ACT.Gelu).then_inc(h_read, 1)
                if s.on(-1):
                    wait(act, x_written, s, i + 2, 1)
                    if i >= 1:
                        wait(act, h_written, s, i, 1)
                    act.activation(xgT[(i + 1) % 2][:], psX[(i + 1) % 2][:, 0:P], ACT.Copy).then_inc(x_read, 1)
            each_tile(act, tile_slot)

        @block.vector
        def _(dve):
            for a in AB:
                for k in range(2):
                    dve.memset(v[a][k][:, :, HD:HD + 1], 1.0).then_inc(zero_done, 1)
                    for st in stack[a][k]:
                        dve.memset(st[:], 0.0).then_inc(stack_zero, 1)
            for k in range(2):
                dve.memset(R[k][:, :, D + 3:D + 4], 0.0)
                dve.memset(R[k][:, 0, D + 1:D + 2], 1.0)
                dve.memset(R[k][:, 1, D + 1:D + 2], 0.0).then_inc(R_set, 1)
            dve.wait_ge(ld_const, 16 * NLOAD)
            dve.tensor_scalar(base[:], cst[:, C_I8:C_I8 + E], float(REGION), None, ALU.mult).then_inc(base_set, 1)
            dve.tensor_copy(dstf[:], cst[:, C_DST:C_DST + 2]).then_inc(base_set, 1)
            dve.wait_ge(base_set, 2)
            dve.wait_ge(ld_b, 32)
            rest = bt
            for k in range(3):
                dve.tensor_copy(bpart[k][:], rest[:]).then_inc(b_split, 1)
                dve.wait_ge(b_split, 2 * k + 1)
                if k < 2:
                    dve.tensor_tensor(brest[k][:], rest[:], bpart[k][:], ALU.subtract).then_inc(b_split, 1)
                    dve.wait_ge(b_split, 2 * k + 2)
                    rest = brest[k]
            dve.wait_ge(radd_mm, 1)
            for k, a in enumerate(AB):
                dve.tensor_tensor(radd[a][:], ml[:, k * D:k * D + D], rr[pre[a] + "bo"], ALU.add).then_inc(radd_done, 1)
            dve.wait_ge(radd_done, 2)
            dve.tensor_tensor(radd["C"][:], radd["C"][:], rr["ln1_b"], ALU.add).then_inc(radd_done, 1)

            def maxima(s, a, j):
                wait(dve, s1_written, s, S1.before(s, a, j) + 1, S1.rate)
                if j == 0 and s.i - LAG1[a] >= 2:
                    wait(dve, mt_written, s, MT.before(Slot(s.i - 2 - LAG1[a] + LAG2[a]), "mt" + a) + 1, MT.rate)
                dve.tensor_reduce(nmax[a][s.par(LAG1[a])][:, HG * j:HG * j + HG],
                                  ps1[j % 2][:].rearrange("p (h k) -> p h k", h=HG), AX.X, ALU.max,
                                  negate=True).then_inc(s1_read, 1)

            def less(s, a, part):
                k, b = s.par(PROJ[a]), s.i - PROJ[a]
                wait(dve, cast[a], s, 2 * b + part + 1, 2)
                if part == 1:
                    wait(dve, left[a], s, 2 * b + 1, 2)
                dve.tensor_tensor(remain[a][k][:] if part == 0 else parts[a][k][:, :, 2, :],
                                  (qk if part == 0 else remain)[a][k][:], parts[a][k][:, :, part, :],
                                  ALU.subtract).then_inc(left[a], 1)

            def normalise(s, a):
                n = OD.before(s, a)
                wait(dve, av_done, s, AV.before(s, a, G - 1) + 1, AV.rate)
                dve.reciprocal(rden[:].rearrange("p (h o) -> p h o", o=1), odh[:, :, HD:HD + 1]).then_inc(rden_done, 1)
                wait(dve, rden_done, s, n + 1, OD.rate)
                if s.i - WEIGH[a] >= 1:
                    wait(dve, mt_written, s, MT.before(Slot(s.i - 1), "ot" + a) + 1, MT.rate)
                dve.tensor_tensor(o[a][:].rearrange("p (h d) -> p h d", h=H), odh[:, :, 0:HD],
                                  rden[:].rearrange("p (h o) -> p h o", o=1).broadcast_to([P, H, HD]),
                                  ALU.mult).then_inc(od_read, 1)

            def residual(s, a):
                b, k = s.i - END[a], s.par(END[a])
                n = ML.before(s, "wo" + a)
                wait(dve, ml_written, s, n + 1, ML.rate)
                wait(dve, xb_done[a], s, b + 1, 1)
                dve.tensor_tensor(res[a][k][:], ml[:, 0:D], xb[a][k][:], ALU.add).then_inc(ml_read, 1)
                wait(dve, ml_read, s, n + 1, ML.rate)
                dve.bn_stats(stat[a][k][:], res[a][k][:]).then_inc(ln_dve[a], 1)
                wait(dve, ln_dve[a], s, 5 * b + 1, 5)
                dve.bn_aggr(mv[a][k][:], stat[a][k][:]).then_inc(ln_dve[a], 2)

            def normal(s, a):
                b, k = s.i - END[a], s.par(END[a])
                wait(dve, ln_pool[a], s, 2 * b + 2, 2)
                wait(dve, ln_dve[a], s, 5 * b + 3, 5)
                dve.tensor_scalar(z[a][k][:], res[a][k][:], mv[a][k][:, 0:1], rstd[a][k][:],
                                  ALU.subtract, ALU.mult).then_inc(ln_dve[a], 1)

            def affine(s, a):
                k, p = s.par(ROWL[a]), {"S": "ln1_", "C": "ln2_"}[a]
                n = ML.before(s, "zt" + a)
                wait(dve, ml_written, s, n + 1, ML.rate)
                dst = (x1T if a == "S" else x2T)[k]
                dve.tensor_scalar(dst[:], ml[:, 0:P], cb[p + "g"], cb[p + "b"], ALU.mult, ALU.add).then_inc(ml_read, 1)
                wait(dve, ml_read, s, n + 1, ML.rate)
                dve.memset(done[a][:], 0.0).then_inc(ln_dve[a], 1)

            def chain(s, lag, n):
                wait(dve, rt_dve, s, RT * (s.i - lag) + n, RT)

            def router_in(s):
                n, k = ML.before(Slot(s.i - 1), "log"), s.par(RL)
                wait(dve, ml_written, s, n + 1, ML.rate)
                dve.tensor_tensor(lg[k][:], ml[:, 0:E], rbt[:], ALU.add).then_inc(ml_read, 1)
                wait(dve, ml_read, s, n + 1, ML.rate)
                dve.tensor_reduce(neg[k][:], lg[k][:], AX.X, ALU.max, negate=True).then_inc(rt_dve, 2)

            def router_top(s):
                k = s.par(RL)
                wait(dve, rt_act, s, 2 * (s.i - RL) + 1, 2)
                dve.reciprocal(rsum[k][:], esum[k][:]).then_inc(rt_dve, 1)
                chain(s, RL, 3)
                dve.tensor_scalar(prob[k][:], ex[k][:], rsum[k][:], None, ALU.mult).then_inc(rt_dve, 1)
                chain(s, RL, 4)
                dve.tensor_tensor(ride[:], neg[k][:], neg[k][:], ALU.add)
                dve.max(pmax[k][:], prob[k][:]).then_inc(rt_dve, 1)
                chain(s, RL, 5)
                dve.tensor_tensor(ride[:], neg[k][:], neg[k][:], ALU.add)
                dve.max_index(pidx[k][:], pmax[k][:], prob[k][:]).then_inc(rt_dve, 1)
                chain(s, RL, 6)
                dve.tensor_copy(pidf[k][:], pidx[k][:, 0:2]).then_inc(rt_dve, 1)
                chain(s, RL, 7)
                dve.tensor_tensor(hot[k][:], cst[:, C_I8:C_I8 + E].rearrange("p (o e) -> p o e", o=1).broadcast_to([P, 2, E]),
                                  pidf[k][:].rearrange("p (c o) -> p c o", o=1).broadcast_to([P, 2, E]),
                                  ALU.is_equal).then_inc(rt_dve, 1)
                chain(s, RL, 8)
                dve.tensor_tensor(picked[k][:], hot[k][:, 0, :], hot[k][:, 1, :], ALU.add).then_inc(rt_dve, 1)

            def router_out(s):
                n, k, b = ML.before(s, "pre"), s.par(RL), s.i - RL
                if b >= 2:
                    wait(dve, scattered[k], s, 32 * (b // 2), 16)
                wait(dve, rt_act, s, 2 * b + 2, 2)
                dve.tensor_scalar(wden[k][:], e2[k][:], 1.0, None, ALU.add).then_inc(rt_dve, 1)
                chain(s, RL, 10)
                dve.reciprocal(R[k][:, 0, D:D + 1], wden[k][:]).then_inc(rt_dve, 1)
                chain(s, RL, 11)
                dve.tensor_tensor(R[k][:, 1, D:D + 1], R[k][:, 0, D:D + 1], e2[k][:], ALU.mult).then_inc(rt_dve, 1)
                dve.tensor_copy(R[k][:, :, D + 2:D + 3].bitcast(U32), dstf[:].rearrange("p (c o) -> p c o", o=1)).then_inc(rt_dve, 1)
                chain(s, RL, 13)
                dve.tensor_scalar(dstf[:], dstf[:], float(2 * P), None, ALU.add).then_inc(rt_dve, 1)
                wait(dve, ml_written, s, n + 1, ML.rate)
                dve.tensor_tensor(place[k][:], ml[:, 0:E], base[:], ALU.add).then_inc(rt_dve, 1)
                chain(s, RL, 15)
                dve.tensor_tensor(base[:], ml[:, E:2 * E], base[:], ALU.add).then_inc(ml_read, 1)
                dve.tensor_tensor(hotp[k][:], hot[k][:], place[k][:].rearrange("p (o e) -> p o e", o=1).broadcast_to([P, 2, E]),
                                  ALU.mult).then_inc(rt_dve, 1)
                chain(s, RL, 16)
                dve.tensor_reduce(rowf[k][:], hotp[k][:], AX.X, ALU.add).then_inc(rt_dve, 1)
                chain(s, RL, 17)
                dve.tensor_copy(rown[k][:], rowf[k][:]).then_inc(rt_dve, 1)
                chain(s, RL, 18)

            def slot(s):
                def run(lag, f, *args):
                    if s.on(lag):
                        f(s, *args)
                run(8, router_in)
                run(6, normalise, "C")
                run(0, less, "S", 0)
                run(5, maxima, "C", 0)
                run(5, maxima, "C", 1)
                run(0, less, "S", 1)
                run(4, less, "C", 0)
                run(5, maxima, "C", 2)
                run(4, less, "C", 1)
                run(5, maxima, "C", 3)
                run(8, router_top)
                run(3, residual, "S")
                run(7, affine, "C")
                run(6, residual, "C")
                run(2, normalise, "S")
                run(1, maxima, "S", 0)
                run(1, maxima, "S", 1)
                run(3, normal, "S")
                run(1, maxima, "S", 2)
                run(6, normal, "C")
                run(1, maxima, "S", 3)
                run(8, router_out)
                run(3, affine, "S")
            each_slot(dve, slot)
            plan_tiles(dve)

            def tile_slot(s):
                if s.on(1):
                    wait(dve, ht_written, s, s.i, 1)
                    if s.i - 1 >= 2:
                        wait(dve, y_written, s, s.i - 2, 1)
                    dve.tensor_copy(hT[(s.i - 1) % 2][:], psT[(s.i - 1) % 2][:]).then_inc(ht_read, 1)
                if s.on(2):
                    i = s.i - 2
                    wait(dve, y_written, s, i + 1, 1)
                    wait(dve, xf_done, s, i + 1, 1)
                    if i >= RING:
                        wait(dve, y_sent[i % RING], s, 16 * (i // RING), 16 // RING)
                    dve.scalar_tensor_tensor(out=ysb[i % RING][:], in0=psY[i % 2][:, 0:D], scalar=xg[i % RING][:, D:D + 1],
                                             in1=xf[i % RING][:], op0=ALU.mult, op1=ALU.add).then_inc(y_done, 1)
            each_tile(dve, tile_slot)

            for q in range(NQ):
                k = q % 2
                dve.wait_ge(y_back[k], 16 * (q // 2 + 1))
                if q >= 2:
                    dve.wait_ge(fin_pool, 2 * (q - 1))
                dve.tensor_tensor(ysum[k][:], yin[k][:, :, 0, :], yin[k][:, :, 1, :], ALU.add).then_inc(fin_dve, 1)
                dve.wait_ge(fin_dve, 4 * q + 1)
                for c in range(4):
                    ins = dve.bn_stats(fstat[k][:, c, :], ysum[k][:, c, :])
                ins.then_inc(fin_dve, 1)
                dve.wait_ge(fin_dve, 4 * q + 2)
                for c in range(4):
                    ins = dve.bn_aggr(fmv[k][:, c, :], fstat[k][:, c, :])
                ins.then_inc(fin_dve, 1)
                dve.wait_ge(fin_dve, 4 * q + 3)
                dve.wait_ge(fin_rstd, 2 * q + 2)
                for c in range(4):
                    ins = dve.tensor_scalar(ysum[k][:, c, :], ysum[k][:, c, :], fmv[k][:, c, 0:1], frstd[k][:, c:c + 1],
                                            ALU.subtract, ALU.mult)
                ins.then_inc(fin_dve, 1)
                dve.wait_ge(fin_dve, 4 * q + 4)
                if q >= 2:
                    dve.wait_ge(stored[k], 16 * (q // 2))
                dve.tensor_tensor(yg[k][:], ysum[k][:], row4("ln3_g"), ALU.mult).then_inc(fin_g, 1)

        @block.gpsimd
        def _(pool):
            pool.memset(nhalf[:], -0.5).then_inc(cast_done, 1)
            pool.memset(eps[:], EPS).then_inc(cast_done, 1)
            pool.wait_ge(ld_const, 16 * NLOAD)
            for dst, c, w in ((identb[:], C_ID, P), (upb[:], C_UP, P), (onesb[:], C_ONE, P),
                              (negmask[:].rearrange("p h q -> p (h q)"), C_CM, HG * P)):
                pool.tensor_copy(dst, cst[:, c:c + w]).then_inc(cast_done, 1)
            pool.wait_ge(cast_done, NCAST)
            pool.wait_ge(radd_done, 3)
            pool.memset(blank[:], 0.0).then_inc(blank_set, 1)
            pool.iota(blank_dst[:], pattern=[[P, NE]], base=2 * TOK, channel_multiplier=1).then_inc(blank_set, 1)
            pool.wait_ge(blank_set, 2)
            pool.tensor_copy(blank[:, :, D + 2:D + 3].bitcast(U32), blank_dst[:].rearrange("p (n o) -> p n o", o=1))\
                .then_inc(blank_set, 1)

            def causal(s, j):
                wait(pool, sel_done, s, G * (s.i - 2) + j, G)
                wait(pool, s2_read, s, S2.before(s, "S", j) + 1, S2.rate)
                pool.tensor_tensor(carrier[:], nhalf[:], nhalf[:], ALU.mult)
                pool.affine_select(out=pT["S"][j][:], in_=pT["S"][j][:], compare_op=ALU.is_ge, fill=0.0, base=0,
                                   pattern=[[0, HG], [1, P]], channel_multiplier=-1).then_inc(sel_done, 1)

            def part(s, a, n):
                b, k = s.i - PROJ[a], s.par(PROJ[a])
                if n == 0:
                    wait(pool, mq_read, s, MQ.before(s, "proj" + a) + 1, MQ.rate)
                    if b >= 2:
                        wait(pool, parts_out[a][k], s, 16 * (b // 2), 8)
                else:
                    wait(pool, left[a], s, 2 * b + 1, 2)
                wait(pool, cast[a], s, 2 * b - 1 + n, 2)
                pool.tensor_tensor(part_ride[a][n][:], nhalf[:], nhalf[:], ALU.mult)
                pool.tensor_copy(parts[a][k][:, :, n, :], (qk if n == 0 else remain)[a][k][:]).then_inc(cast[a], 1)

            def inv_std(s, a):
                b, k = s.i - END[a], s.par(END[a])
                wait(pool, ln_dve[a], s, 5 * b + 3, 5)
                pool.tensor_tensor(ve[a][k][:], mv[a][k][:, 1:2], eps[:], ALU.add).then_inc(ln_pool[a], 1)
                wait(pool, ln_pool[a], s, 2 * b + 1, 2)
                pool.tensor_tensor(rstd[a][k][:], ve[a][k][:], nhalf[:], ALU.pow).then_inc(ln_pool[a], 1)

            def rows_out(s, a):
                b, k = s.i - ROWL[a], s.par(ROWL[a])
                wait(pool, ln_dve[a], s, 5 * b + 4, 5)
                if a == "S" and b >= 2:
                    wait(pool, xb_done["C"], s, b - 1, 1)
                g = rr["ln1_g" if a == "S" else "ln2_g"]
                pool.tensor_tensor(zg[a][k][:], z[a][k][:], g, ALU.mult).then_inc(row_pool[a], 1)
                if a == "C":
                    wait(pool, row_pool[a], s, 3 * b + 1, 3)
                    if b >= 2:
                        wait(pool, scattered[k], s, 32 * (b // 2), 16)
                    for c in range(2):
                        pool.tensor_tensor(R[k][:, c, 0:D], zg[a][k][:], rr["ln2_b"], ALU.add).then_inc(row_pool[a], 1)

            def base_rows(s, a):
                lag = 2 if a == "S" else 5
                b, k = s.i - lag, s.par(lag)
                if a == "S":
                    wait(pool, ld_r[k], s, 16 * (b // 2 + 1), 8)
                else:
                    wait(pool, row_pool["S"], s, b + 1, 1)
                if b >= 2:
                    wait(pool, ln_dve[a], s, 5 * (b - 2) + 1, 5)
                pool.tensor_tensor(xb[a][k][:], xr[k][:] if a == "S" else zg["S"][k][:], radd[a][:], ALU.add)\
                    .then_inc(xb_done[a], 1)

            def scatter(s):
                k = s.par(SL)
                wait(pool, rode, s, s.i - SL, 1)
                wait(pool, row_pool["C"], s, 3 * (s.i - SL) + 3, 3)
                wait(pool, rt_dve, s, RT * (s.i - SL) + 18, RT)
                pool.tensor_tensor(ride_pool[:], nhalf[:], nhalf[:], ALU.mult).then_inc(rode, 1)
                for c in range(2):
                    pool.indirect_dma_start(out=xs, out_offset=bass.IndirectOffsetOnAxis(ap=rown[k][:, c:c + 1], axis=0),
                                            in_=R[k][:, c, :], in_offset=None).then_inc(scattered[k], 16)

            def slot(s):
                def run(lag, f, *args):
                    if s.on(lag):
                        f(s, *args)
                run(9, scatter)
                run(0, part, "S", 0)
                run(0, part, "S", 1)
                run(4, part, "C", 0)
                run(4, part, "C", 1)
                run(2, causal, 0)
                run(2, causal, 1)
                run(2, causal, 2)
                run(2, causal, 3)
                run(3, inv_std, "S")
                run(6, inv_std, "C")
                run(5, base_rows, "C")
                run(2, base_rows, "S")
                run(3, rows_out, "S")
                run(7, rows_out, "C")
            each_slot(pool, slot)

            pool.wait_ge(plan_dve, 2)
            for e in range(E):
                pool.indirect_dma_start(out=xs, out_offset=bass.IndirectOffsetOnAxis(ap=padn[:, e:e + 1], axis=0),
                                        in_=blank[:, e, :], in_offset=None).then_inc(padded, 16)

            def tile_slot(s):
                if s.on(2):
                    wait(pool, y_done, s, s.i - 1, 1)
                if s.on(0):
                    i = s.i
                    wait(pool, xg_in[i % RING], s, 16 * (i // RING + 1), 16 // RING)
                    if i >= RING:
                        wait(pool, y_done, s, i - RING + 1, 1)
                    pool.tensor_tensor(xf[i % RING][:], xg[i % RING][:, 0:D], xg[i % RING][:, D + 1:D + 2].broadcast_to([P, D]),
                                       ALU.mult).then_inc(xf_done, 1)
                if s.on(2):
                    i = s.i - 2
                    pool.indirect_dma_start(out=ys, out_offset=bass.IndirectOffsetOnAxis(
                        ap=xg[i % RING][:, D + 2:D + 3].bitcast(U32), axis=0), in_=ysb[i % RING][:, :], in_offset=None)\
                        .then_inc(y_sent[i % RING], 16)
            each_tile(pool, tile_slot)

            for q in range(NQ):
                k = q % 2
                pool.wait_ge(fin_dve, 4 * q + 3)
                pool.tensor_tensor(fve[k][:], fmv[k][:, :, 1], eps[:].broadcast_to([P, 4]), ALU.add).then_inc(fin_rstd, 1)
                pool.wait_ge(fin_rstd, 2 * q + 1)
                pool.tensor_tensor(frstd[k][:], fve[k][:], nhalf[:].broadcast_to([P, 4]), ALU.pow).then_inc(fin_rstd, 1)
                pool.wait_ge(fin_g, q + 1)
                pool.tensor_tensor(yg[k][:], yg[k][:], row4("ln3_b"), ALU.add).then_inc(fin_pool, 2)


NCAST, NPLAN = 6, 15


def constants():
    import numpy as np
    c = np.zeros((P, NCONST), np.float32)
    p = np.arange(P)
    c[:, C_ID:C_ID + P] = np.eye(P)
    for h in range(HG):
        c[:, C_CM + h * P:C_CM + h * P + P] = np.where(p[None, :] > p[:, None], -1e30, 0.0)
    c[:, C_UP:C_UP + P] = p[:, None] < p[None, :]
    c[:, C_ONE:C_ONE + P] = 1.0
    c[:, C_I8:C_I8 + E] = np.arange(E)
    c[:, C_DST:C_DST + 2] = 2 * p[:, None] + np.arange(2)
    c[:, C_I72:C_I72 + TILES] = np.arange(TILES)
    c[:, C_P] = p
    return c


def kernel(**inputs):
    import numpy as np
    import concourse.bacc as bacc
    from concourse.bass_utils import run_bass_kernel_spmd as run

    def arr(name):
        a = np.asarray(inputs["L0_xattn_" + name])
        if name[-2:] in ("wq", "wk", "bq", "bk"):
            a = a.reshape(a.shape[:-1] + (H, HD)).swapaxes(-1, -2).reshape(a.shape)
        return np.ascontiguousarray(a)

    arrays = {
        "x": np.ascontiguousarray(inputs["x"]), "ctx_in": np.ascontiguousarray(inputs["ctx_1024"]),
        "const": constants(), "cols": np.ascontiguousarray(np.stack([arr(n) for n in COLS], 1)),
        "rows": np.stack([arr(n) for n in ROWS]), "mats": np.stack([arr(n) for n in MATS]),
        "rw": arr("router_w"), "rb": arr("router_b"), "w1": arr("e_w1"), "b1": arr("e_b1"),
        "w2": arr("e_w2"), "b2": arr("e_b2"),
    }
    nc = bacc.Bacc("TRN2", target_bir_lowering=False, num_devices=1)
    aps = {n: nc.dram_tensor(n, a.shape, mybir.dt.from_np(a.dtype), kind="ExternalInput").ap() for n, a in arrays.items()}
    out = nc.dram_tensor("out", (B, P, D), F32, kind="ExternalOutput").ap()
    build(nc, out=out, **aps)
    got = run(nc, [arrays], core_ids=[0])
    return got.results[0]["out"]
```

```python
from contextlib import ExitStack

import concourse.bass as bass
from concourse import mybir

F32, BF16 = mybir.dt.float32, mybir.dt.bfloat16
U32, I32 = mybir.dt.uint32, mybir.dt.int32
ALU, ACT, AX = mybir.AluOpType, mybir.ActivationFunctionType, mybir.AxisListType

B, P, D, H, E, FF = 32, 128, 128, 16, 8, 512
HD = D // H
G = 4
HG = H // G
SPLIT = 3
STACK = 7 * HD
READS = 5
SHIFT = P - 1
SCALE = float(HD) ** -0.5
EPS = 1e-5
TOK = B * P
ROW = D + 4
TILES = (2 * TOK + E * (P - 1)) // P + 1
SPARE = TILES - 2 * TOK // P
REGION = TOK + P
FC = FF // P
RING, RUNUP = 8, 5

C_ID, C_UP, C_ONE, C_CM, C_I8 = 0, P, 2 * P, 3 * P, 7 * P
C_DST, C_I72 = C_I8 + E, C_I8 + E + 2
C_HM, NCONST = C_I72 + TILES, C_I72 + TILES + HG
COLS = ["sa_bq", "sa_bk", "sa_bv", "ca_bq", "ca_bk", "ca_bv", "ln1_g", "ln1_b", "ln2_g", "ln2_b"]
ROWS = ["sa_bo", "ca_bo", "ln1_g", "ln1_b", "ln2_g", "ln2_b", "ln3_g", "ln3_b"]
MATS = ["sa_wq", "sa_wk", "sa_wv", "sa_wo", "ca_wq", "ca_wk", "ca_wv", "ca_wo"]

LO, LOOP = 10, 10
FIRST, LAST = -1, B + 8


class Slot:

    def __init__(self, i, t=None, step=2, n=B):
        self.i, self.t, self.step, self.n = i, t, step, n

    def on(self, lag):
        return 0 <= self.i - lag < self.n

    def par(self, lag):
        return (self.i - lag) % 2

    def value(self, v, per_slot):
        return v if self.t is None else v + self.t * (self.step * per_slot)

    def batch(self, lag):
        return self.value(self.i - lag, 1)


class Turns:

    def __init__(self, *kinds):
        self.kinds = kinds
        self.rate = sum(n for _, _, n in kinds)

    def before(self, s, kind):
        n = sum(k for i in range(FIRST, s.i) for _, lag, k in self.kinds if 0 <= i - lag < B)
        for name, lag, k in self.kinds:
            if name == kind:
                return n
            n += k * s.on(lag)

    def total(self):
        return B * self.rate


def wait(eng, sem, s, v, rate):
    if v > 0:
        eng.wait_ge(sem, s.value(v, rate))


def each_slot(eng, body, first=FIRST):
    for i in range(first, LO):
        body(Slot(i))
    with eng.Fori(0, LOOP) as t:
        for u in range(2):
            body(Slot(LO + u, t))
    for i in range(LO + 2 * LOOP, LAST):
        body(Slot(i))


def each_tile(eng, body):
    for i in range(-RUNUP, RING):
        body(Slot(i, None, RING, TILES))
    with eng.Fori(0, TILES // RING - 2) as t:
        for u in range(RING):
            body(Slot(RING + u, t, RING, TILES))
    for i in range(TILES - RING, TILES + 3):
        body(Slot(i, None, RING, TILES))


MQ = Turns(("projC", 4, 1), ("ztC", 7, 1), ("mtC", 5, 1), ("projS", 0, 1), ("ztS", 3, 1),
           ("vC", 5, 1), ("vS", 1, 1), ("mtS", 1, 1), ("trx", -1, 1), ("trc", 3, 1))
ML = Turns(("woS", 3, 1), ("log", 7, 1), ("woC", 6, 1), ("pre", 7, 1))
S1 = Turns(("C", 5, G), ("S", 1, G))
S2 = Turns(("S", 2, G), ("C", 5, G))
OD = Turns(("C", 6, 1), ("S", 2, 1))
PROJ, VAL, LAG1, TURN1 = {"S": 0, "C": 4}, {"S": 1, "C": 5}, {"S": 1, "C": 5}, {"S": 1, "C": 5}
LAG2, WEIGH = {"S": 2, "C": 5}, {"S": 2, "C": 6}
END, ROWL, RL, SL = {"S": 3, "C": 6}, {"S": 3, "C": 7}, 7, 8


def build(nc, x, ctx_in, const, cols, rows, mats, rw, rb, w1, w2, b2, out):
    with ExitStack() as ctx:
        def sb(name, shape, dt=F32):
            return ctx.enter_context(nc.sbuf_tensor(name, shape, dt))

        def sem(name):
            return ctx.enter_context(nc.semaphore(name))

        AB = ("S", "C")
        cst = sb("cst", [P, NCONST])
        ident = cst[:, C_ID:C_ID + P]
        ones = cst[:, C_ONE:C_ONE + P]
        identb, upb, onesb = (sb(n, [P, P], BF16) for n in ("identb", "upb", "onesb"))
        negmask = sb("negmask", [P, HG, P], BF16)
        col = sb("col", [P, len(COLS)])
        row = sb("row", [P, len(ROWS), D])
        mat = sb("mat", [P, len(MATS), D])
        rwt, rbt = sb("rwt", [P, E]), sb("rbt", [P, E])
        radd = {a: sb(f"radd{a}", [P, D]) for a in AB}
        xin = [sb(f"xin{k}", [P, D]) for k in range(2)]
        cin = [sb(f"cin{k}", [P, D]) for k in range(2)]
        xT = [sb(f"xT{k}", [P, P]) for k in range(2)]
        cT = [sb(f"cT{k}", [P, P]) for k in range(2)]
        x1T = [sb(f"x1T{k}", [P, P]) for k in range(2)]
        x2T = [sb(f"x2T{k}", [P, P]) for k in range(2)]

        def two(name, shape, dt=F32):
            return {a: [sb(f"{name}{a}{k}", shape, dt) for k in range(2)] for a in AB}
        qk = two("qk", [P, 2, P])
        parts, remain = two("parts", [P, 2, SPLIT, P], BF16), two("remain", [P, 2, P])
        stack = {a: [[sb(f"{n}stack{a}{k}", [P, H, P], BF16) for n in "kq"] for k in range(2)] for a in AB}
        v = two("v", [P, D])
        nmax, nmaxT = two("nmax", [P, H], BF16), two("nmaxT", [H, P], BF16)
        pT = {a: [sb(f"pT{a}{j}", [P, HG, P]) for j in range(G)] for a in AB}
        parts_d = {a: [nc.dram_tensor(f"parts_d{a}{k}", (2, SPLIT * HD, H * P), BF16, kind="Internal").ap()
                       for k in range(2)] for a in AB}
        rden = sb("rden", [P, P])
        oT = {a: sb(f"oT{a}", [P, HG, P]) for a in AB}
        wom = {a: sb(f"wom{a}", [P, HG, D]) for a in AB}
        onem = sb("onem", [P, HG, 32])
        xr = [sb(f"xr{k}", [P, D]) for k in range(2)]
        xb = two("xb", [P, D])
        res, stat, mv = two("res", [P, D]), two("stat", [P, 6]), two("mv", [P, 2])
        ve, rstd, z = two("ve", [P, 1]), two("rstd", [P, 1]), two("z", [P, D])
        zg = two("zg", [P, D])
        nhalf, carrier, eps = sb("nhalf", [P, 1]), sb("carrier", [P, 1]), sb("eps", [P, 1])

        def ps(name, dt=F32, n=512):
            return ctx.enter_context(nc.psum_tensor(name, [P, n], dt))
        ps1, ps2 = [ps("ps1a"), ps("ps1b")], [ps("ps2a"), ps("ps2b")]
        po, pd, mq, ml = ps("po"), ps("pd"), ps("mq"), ps("ml")
        mtb = mq[0:H, 0:P // 2].bitcast(BF16)

        ld_const, ld_rows = sem("ld_const"), sem("ld_rows")
        ld_x, ld_c, ld_r = ([sem(f"{n}{k}") for k in range(2)] for n in ("ld_x", "ld_c", "ld_r"))
        cast_done, radd_mm, radd_done = sem("cast_done"), sem("radd_mm"), sem("radd_done")
        mq_written, mq_read = sem("mq_written"), sem("mq_read")
        ml_written, ml_read = sem("ml_written"), sem("ml_read")
        s1_written, s1_read, s2_written, s2_read = map(sem, ("s1_written", "s1_read", "s2_written", "s2_read"))
        av_done, od_read = sem("av_done"), sem("od_read")
        rden_done = sem("rden_done")
        cast = {a: sem(f"cast{a}") for a in AB}
        left = {a: sem(f"left{a}") for a in AB}
        parts_out, stack_in, row_in = ({a: [sem(f"{n}{a}{k}") for k in range(2)] for a in AB}
                                       for n in ("parts_out", "stack_in", "row_in"))
        stack_zero, stack_ones = sem("stack_zero"), sem("stack_ones")
        ln_dve = {a: sem(f"ln_dve{a}") for a in AB}
        ln_pool = {a: sem(f"ln_pool{a}") for a in AB}
        row_pool = {a: sem(f"row_pool{a}") for a in AB}
        sel_done = sem("sel_done")
        xb_done = {a: sem(f"xb_done{a}") for a in AB}

        R = [sb(f"R{k}", [P, 2, ROW]) for k in range(2)]

        def pair(name, shape, dt=F32):
            return [sb(f"{name}{k}", shape, dt) for k in range(2)]
        lg, neg, ex = pair("lg", [P, E]), pair("neg", [P, 1]), pair("ex", [P, E])
        esum, rsum, prob, pmax = pair("esum", [P, 1]), pair("rsum", [P, 1]), pair("prob", [P, E]), pair("pmax", [P, E])
        pidx, pidf, hot = pair("pidx", [P, E], U32), pair("pidf", [P, 2]), pair("hot", [P, 2, E])
        picked, e2, wden = pair("picked", [P, E], BF16), pair("e2", [P, 1]), pair("wden", [P, 1])
        place, hotp, rowf, rown = pair("place", [P, E]), pair("hotp", [P, 2, E]), pair("rowf", [P, 2]), pair("rown", [P, 2], U32)
        ride, ride_pool = sb("ride", [P, 1]), sb("ride_pool", [P, 1])
        base, dstf = sb("base", [P, E]), sb("dstf", [P, 2])
        xs = nc.dram_tensor("xs", (E * REGION + SPARE * P, ROW), F32, kind="Internal").ap()
        ys = nc.dram_tensor("ys", (2 * TOK + (E + SPARE) * P, D), F32, kind="Internal").ap()
        RT = 18
        rt_dve, rt_act = sem("rt_dve"), sem("rt_act")
        scattered = [sem(f"scattered{k}") for k in range(2)]
        rode = sem("rode")
        R_set, base_set = sem("R_set"), sem("base_set")
        NE = E + SPARE
        blank = sb("blank", [P, NE, ROW])
        blank_dst = sb("blank_dst", [P, NE], U32)
        plan_dve, blank_set, padded, spare_set = sem("plan_dve"), sem("blank_set"), sem("padded"), sem("spare_set")
        cnt, cnti, nt = sb("cnt", [P, E]), sb("cnti", [P, E], I32), sb("nt", [P, E])
        cum, delta = sb("cum", [P, E]), sb("delta", [P, E])
        padn = sb("padn", [P, E], I32)
        past, pastd = sb("past", [P, TILES, E]), sb("pastd", [P, TILES, E])
        tef, trf = sb("tef", [P, TILES]), sb("trf", [P, TILES])
        tile_e, tile_r = sb("tile_e", [P, TILES], I32), sb("tile_r", [P, TILES], I32)
        w2t = sb("w2t", [P, E, FC, D])
        bt = sb("bt", [E, D])
        bpart = [sb(f"bpart{k}", [E, D], BF16) for k in range(3)]
        brest = [sb("brest0", [E, D]), bt]
        bp = sb("bp", [3, E, D], BF16)
        bd = nc.dram_tensor("bd", (3, E, D), BF16, kind="Internal").ap()
        ld_w, ld_b, b_split, b_stored, b_moved = map(sem, ("ld_w", "ld_b", "b_split", "b_stored", "b_moved"))
        xg = [sb(f"xg{k}", [P, ROW]) for k in range(RING)]
        w1g = [sb(f"w1g{k}", [P, FF + FC]) for k in range(RING)]
        xgT, hT = pair("xgT", [P, P]), pair("hT", [P, FF])
        xf, ysb = [sb(f"xf{k}", [P, D]) for k in range(RING)], [sb(f"ysb{k}", [P, D]) for k in range(RING)]
        psX, psH, psY = [mq, ml], ps1, [po, pd]
        xg_in, w1_in = ([sem(f"{n}{k}") for k in range(RING)] for n in ("xg_in", "w1_in"))
        y_sent = [sem(f"y_sent{k}") for k in range(RING)]
        x_written, x_read, h_written, h_read = map(sem, ("x_written", "x_read", "h_written", "h_read"))
        y_written, y_done, xf_done = map(sem, ("y_written", "y_done", "xf_done"))
        NQ, NF = B // 4, 4

        def four(name, shape):
            return [sb(f"{name}{k}", shape) for k in range(NF)]
        yin, yout = four("yin", [P, 4, 2, D]), four("yout", [P, 4, D])
        fstat, fmv, fve = four("fstat", [P, 4, 6]), four("fmv", [P, 4, 2]), four("fve", [P, 4])
        frstd, fshift = four("frstd", [P, 4]), four("fshift", [P, 4])
        y_back, stored = [sem(f"y_back{k}") for k in range(NF)], [sem(f"stored{k}") for k in range(NF)]
        fin_dve, fin_rstd, fin_shift, fin_z, fin_g, fin_pool = map(sem, (
            "fin_dve", "fin_rstd", "fin_shift", "fin_z", "fin_g", "fin_pool"))

        def row4(name):
            return rr[name].rearrange("p (o d) -> p o d", o=1).broadcast_to([P, 4, D])

        def plan_tiles(dve):
            n = [0]

            def step(ins):
                ins.then_inc(plan_dve, 1)
                n[0] += 1
                dve.wait_ge(plan_dve, n[0])

            def over(ap):
                return ap.rearrange("p (o e) -> p o e", o=1).broadcast_to([P, TILES, E])
            step(dve.tensor_copy(padn[:], base[:]))
            step(dve.tensor_scalar(cnt[:], cst[:, C_I8:C_I8 + E], -float(REGION), float(P - 1), ALU.mult, ALU.add))
            step(dve.tensor_tensor(cnt[:], cnt[:], base[:], ALU.add))
            step(dve.tensor_copy(cnti[:], cnt[:]))
            step(dve.tensor_scalar(cnti[:], cnti[:], 7, None, ALU.arith_shift_right))
            step(dve.tensor_copy(nt[:], cnti[:]))
            step(dve.tensor_tensor_scan(cum[:], ones[:, 0:E], nt[:], 0.0, ALU.mult, ALU.add))
            step(dve.tensor_scalar(delta[:], nt[:], -float(P), float(REGION), ALU.mult, ALU.add))
            step(dve.tensor_tensor(past[:], cst[:, C_I72:C_I72 + TILES].rearrange("p (i o) -> p i o", o=1)
                                   .broadcast_to([P, TILES, E]), over(cum[:]), ALU.is_ge))
            step(dve.tensor_reduce(tef[:], past[:], AX.X, ALU.add))
            step(dve.tensor_scalar(tile_e[:], tef[:], float(E - 1), None, ALU.min))
            step(dve.tensor_tensor(pastd[:], past[:], over(delta[:]), ALU.mult))
            step(dve.tensor_reduce(trf[:], pastd[:], AX.X, ALU.add))
            step(dve.scalar_tensor_tensor(out=tile_r[:], in0=cst[:, C_I72:C_I72 + TILES], scalar=float(P), in1=trf[:],
                                          op0=ALU.mult, op1=ALU.add))
            assert n[0] == NPLAN

        def pad(eng, experts):
            eng.wait_ge(plan_dve, 1)
            for e in experts:
                r = eng.value_load(padn[0:1, e:e + 1], min_val=0, max_val=E * REGION - P)
                eng.dma_start(xs[bass.ds(r, P), :], blank[:, e, :]).then_inc(padded, 16)

        cb = {n: col[:, k:k + 1] for k, n in enumerate(COLS)}
        rr = {n: row[:, k, :] for k, n in enumerate(ROWS)}
        W = {n: mat[:, k, :] for k, n in enumerate(MATS)}
        pre = {"S": "sa_", "C": "ca_"}
        NLOAD, NROWS = 3, 3

        block = ctx.enter_context(nc.Block())

        @block.sync
        def _(sp):
            for dst, src in ((cst[:], const), (col[:], cols), (mat[:], mats.rearrange("m p n -> p m n"))):
                sp.dma_start(dst, src).then_inc(ld_const, 16)

            def load_rest():
                for dst, src in ((row[:], rows.rearrange("(o r) d -> o r d", o=1).broadcast_to([P, len(ROWS), D])),
                                 (rwt[:], rw), (rbt[:], rb.rearrange("(o e) -> o e", o=1).broadcast_to([P, E]))):
                    sp.dma_start(dst, src).then_inc(ld_rows, 16)
                sp.dma_start(bt[:], b2).then_inc(ld_b, 16)

            def stack_one():
                sp.wait_ge(cast_done, NCAST)
                for a in AB:
                    for k in range(2):
                        sp.dma_start(stack[a][k][0][SHIFT:P], onesb[0:H, :]).then_inc(stack_ones, 16)

            def experts_in():
                sp.dma_start(w2t[:], w2.rearrange("e (c f) d -> f e c d", f=P)).then_inc(ld_w, 16)
                for k in range(3):
                    sp.wait_ge(b_split, 2 * k + 1)
                    sp.dma_start(bd[k], bpart[k][:]).then_inc(b_stored, 16)

            def biases_in():
                sp.wait_ge(b_stored, 48)
                sp.dma_start(bp[:], bd).then_inc(b_moved, 16)

            def spare_tiles():
                sp.wait_ge(blank_set, 3)
                for u in range(SPARE):
                    sp.dma_start(xs[E * REGION + u * P:E * REGION + (u + 1) * P, :], blank[:, E + u, :]).then_inc(spare_set, 16)

            def shift(s, a):
                k = s.par(TURN1[a])
                wait(sp, mq_read, s, MQ.before(s, "mt" + a) + 1, MQ.rate)
                sp.dma_start(stack[a][k][1][SHIFT:P].rearrange("o h q -> o (h q)"),
                             nmaxT[a][k][:]).then_inc(row_in[a][k], 16)

            def store_parts(s, a):
                k, b = s.par(PROJ[a]), s.i - PROJ[a]
                wait(sp, left[a], s, 2 * b + 2, 2)
                sp.dma_start(parts_d[a][k].rearrange("n (s r) (h t) -> (r h) (n s) t", s=SPLIT, h=H),
                             parts[a][k][:].rearrange("p n s t -> p (n s) t")).then_inc(parts_out[a][k], 16)

            def load_stacks(s, a):
                k, b = s.par(PROJ[a]), s.i - PROJ[a]
                wait(sp, parts_out[a][k], s, 16 * (b // 2 + 1), 8)
                ks, qs = stack[a][k]
                kd, qd = parts_d[a][k][0], parts_d[a][k][1]
                n = SPLIT * HD
                sp.dma_start(ks[0:2 * n],
                             kd.rearrange("(o r) n -> o r n", o=1).broadcast_to([2, n, H * P])).then_inc(stack_in[a][k], 16)
                sp.dma_start(ks[2 * n:STACK], kd[0:HD]).then_inc(stack_in[a][k], 16)
                for u in range(2):
                    sp.dma_start(qs[u * n:u * n + n],
                                 qd[u * HD:u * HD + HD].rearrange("(o r) n -> o r n", o=1)
                                 .broadcast_to([SPLIT, HD, H * P])).then_inc(stack_in[a][k], 16)
                sp.dma_start(qs[2 * n:STACK], qd[2 * HD:n]).then_inc(stack_in[a][k], 16)

            def load(s, lag, src, dst, done):
                sp.dma_start(dst[s.par(lag)][:], src[bass.ds(s.batch(lag), 1)].rearrange("o p d -> (o p) d"))\
                    .then_inc(done[s.par(lag)], 16)

            def slot(s):
                if s.on(-2):
                    if s.on(0):
                        wait(sp, mq_written, s, MQ.before(Slot(s.i - 1), "trx") + 1, MQ.rate)
                    load(s, -2, x, xin, ld_x)
                if s.on(1):
                    if s.i - 1 >= 2:
                        wait(sp, xb_done["S"], s, s.i - 2, 1)
                    load(s, 1, x, xr, ld_r)
                if s.on(4):
                    store_parts(s, "C")
                if s.on(5):
                    shift(s, "C")
                if s.on(4):
                    load_stacks(s, "C")
                if s.on(0):
                    store_parts(s, "S")
                if s.on(2):
                    wait(sp, s2_written, s, S2.before(s, "S") + G, S2.rate)
                    load(s, 2, ctx_in, cin, ld_c)
                if s.on(0):
                    load_stacks(s, "S")
                if s.on(1):
                    shift(s, "S")
            slot(Slot(FIRST - 1))
            load_rest()
            slot(Slot(FIRST))
            sp.wait_ge(stack_zero, 8)
            after = {0: stack_one, 3: experts_in, 5: biases_in, 7: spare_tiles}

            def slot_and_more(s):
                slot(s)
                if s.t is None and s.i in after:
                    after[s.i]()
            each_slot(sp, slot_and_more, FIRST + 1)
            pad(sp, range(E // 2))
            sp.wait_ge(plan_dve, NPLAN)
            sp.wait_ge(padded, 16 * E)
            sp.wait_ge(spare_set, 16 * SPARE)
            for k in range(2):
                sp.wait_ge(scattered[k], 16 * B)

            def tile_slot(s):
                if s.on(-RUNUP):
                    i = s.i + RUNUP
                    if i >= RING:
                        wait(sp, y_sent[i % RING], s, 16 * (i // RING), 16 // RING)
                    at = i if s.t is None else s.value(i, 1)
                    r = sp.value_load(tile_r[0:1, bass.ds(at, 1)], min_val=0, max_val=E * REGION + SPARE * P - P)
                    sp.dma_start(xg[i % RING][:], xs[bass.ds(r, P), :]).then_inc(xg_in[i % RING], 16)
                    e = sp.value_load(tile_e[0:1, bass.ds(at, 1)], min_val=0, max_val=E - 1)
                    sp.dma_start(w1g[i % RING][:], w1[bass.ds(e, 1)].rearrange("o d f -> (o d) f")).then_inc(w1_in[i % RING], 16)
            each_tile(sp, tile_slot)

            for k in range(RING):
                sp.wait_ge(y_sent[k], 16 * TILES // RING)
            for q in range(NQ + 3):
                if q < NQ:
                    if q >= NF:
                        sp.wait_ge(fin_dve, 3 * (q - NF) + 1)
                    sp.dma_start(yin[q % NF][:], ys[8 * P * q:8 * P * (q + 1), :].rearrange("(n p c) d -> p n c d", n=4, c=2))\
                        .then_inc(y_back[q % NF], 16)
                if q >= 3:
                    sp.wait_ge(fin_pool, q - 2)
                    sp.dma_start(out[4 * (q - 3):4 * (q - 2)].rearrange("n p d -> p n d"), yout[(q - 3) % NF][:])\
                        .then_inc(stored[(q - 3) % NF], 16)
            for k in range(NF):
                sp.wait_ge(stored[k], 16 * NQ // NF)

        @block.tensor
        def _(pe):
            pe.wait_ge(ld_const, 16 * NLOAD)
            for k, a in enumerate(AB):
                bv = cb[pre[a] + "bv"]
                mm = pe.matmul(ml[:, k * D:k * D + D], bv.broadcast_to([P, P]), W[pre[a] + "wo"],
                               start=True, stop=True)
            mm.then_inc(radd_mm, 1)

            def max_scores(s, a, j):
                k, b = s.par(LAG1[a]), s.i - LAG1[a]
                if a == "S" and j == 0 and s.t is None and b == 0:
                    pe.wait_ge(radd_done, 2)
                    pe.wait_ge(cast_done, NCAST)
                    pe.wait_ge(stack_ones, 64)
                if j == 0:
                    wait(pe, stack_in[a][k], s, 16 * READS * (b // 2 + 1), 8 * READS)
                wait(pe, s1_read, s, S1.before(s, a) + j - 1, S1.rate)
                ks, qs = stack[a][k]
                for h in range(HG):
                    mm = pe.matmul(ps1[j % 2][:, h * P:h * P + P], qs[0:SHIFT, j * HG + h, :], ks[0:SHIFT, j * HG + h, :],
                                   start=(h == 0 or a == "C"), stop=(a == "C"), skip_group_check=True)
                if a == "S":
                    mm = pe.matmul(ps1[j % 2][:], identb[:], negmask[:], start=False, stop=True, skip_group_check=True)
                mm.then_inc(s1_written, 1)

            def exp_scores(s, a, j):
                k, b = s.par(LAG2[a]), s.i - LAG2[a]
                if j == 0:
                    wait(pe, row_in[a][k], s, 16 * (b // 2 + 1), 8)
                wait(pe, s2_read, s, S2.before(s, a) + j - 1, S2.rate)
                ks, qs = stack[a][k]
                for h in range(HG):
                    mm = pe.matmul(ps2[j % 2][:, h * P:h * P + P], ks[:, j * HG + h, :], qs[:, j * HG + h, :],
                                   start=True, stop=True)
                mm.then_inc(s2_written, 1)

            def weigh(s, a):
                b = s.i - WEIGH[a]
                wait(pe, od_read, s, OD.before(s, a), OD.rate)
                wait(pe, mq_read, s, MQ.before(Slot(s.i - WEIGH[a] + VAL[a]), "v" + a) + 1, MQ.rate)
                if a == "S":
                    wait(pe, sel_done, s, G * b + G, G)
                else:
                    wait(pe, s2_read, s, S2.before(Slot(s.i - WEIGH[a] + LAG2[a]), a) + G, S2.rate)
                for j in range(G):
                    r = slice(32 * j, 32 * j + 32)
                    pe.matmul(po[r, :], v[a][b % 2][:, r], pT[a][j][:], start=True, stop=True)
                for h in range(HG):
                    for j in range(G):
                        mm = pe.matmul(pd[32 * j:32 * j + 32, 0:P], onem[:, h, :], pT[a][j][:, h, :], start=(h == 0),
                                       stop=(h == HG - 1), skip_group_check=True)
                mm.then_inc(av_done, 1)

            def project(s, a):
                wait(pe, mq_read, s, MQ.before(s, "proj" + a), MQ.rate)
                k = s.par(PROJ[a])
                if a == "S":
                    src = kv = xT[k][:]
                else:
                    src, kv = x1T[k][:], cT[k][:]
                p = pre[a]
                pe.matmul(mq[:, 0:P], W[p + "wk"], kv, start=True, stop=True)
                pe.matmul(mq[:, P:2 * P], W[p + "wq"], src, start=True, stop=True).then_inc(mq_written, 1)

            def values(s, a):
                wait(pe, mq_read, s, MQ.before(s, "v" + a), MQ.rate)
                kv = (xT if a == "S" else cT)[s.par(VAL[a])][:]
                pe.matmul(mq[:, 0:D], kv, W[pre[a] + "wv"], start=True, stop=True).then_inc(mq_written, 1)

            def turn(s, what):
                wait(pe, mq_read, s, MQ.before(s, what), MQ.rate)
                lag, src, ld = (-1, xin, ld_x) if what == "trx" else (3, cin, ld_c)
                wait(pe, ld[s.par(lag)], s, 16 * ((s.i - lag) // 2 + 1), 8)
                pe.transpose(mq[:, 0:P], src[s.par(lag)][:], ident).then_inc(mq_written, 1)

            def turn_max(s, a):
                wait(pe, mq_read, s, MQ.before(s, "mt" + a), MQ.rate)
                wait(pe, s1_read, s, S1.before(s, a) + G, S1.rate)
                pe.transpose(mtb, nmax[a][s.par(TURN1[a])][:], identb[:]).then_inc(mq_written, 1)

            def out_proj(s, a):
                wait(pe, ml_read, s, ML.before(s, "wo" + a), ML.rate)
                wait(pe, od_read, s, OD.before(Slot(s.i - END[a] + WEIGH[a]), a) + 1, OD.rate)
                for h in range(HG):
                    mm = pe.matmul(ml[:, 0:D], oT[a][:, h, :], wom[a][:, h, :], start=(h == 0), stop=(h == HG - 1))
                mm.then_inc(ml_written, 1)

            def turn_norm(s, a):
                wait(pe, mq_read, s, MQ.before(s, "zt" + a), MQ.rate)
                wait(pe, ln_dve[a], s, 4 * (s.i - ROWL[a]) + 4, 4)
                pe.transpose(mq[:, 0:P], z[a][s.par(ROWL[a])][:], ident).then_inc(mq_written, 1)

            def logits(s):
                wait(pe, ml_read, s, ML.before(s, "log"), ML.rate)
                wait(pe, mq_read, s, MQ.before(s, "ztC") + 1, MQ.rate)
                pe.matmul(ml[:, 0:E], x2T[s.par(7)][:], rwt[:], start=True, stop=True).then_inc(ml_written, 1)

            def prefix(s):
                wait(pe, ml_read, s, ML.before(s, "pre"), ML.rate)
                wait(pe, rt_dve, s, RT * (s.i - RL) + 9, RT)
                pe.matmul(ml[:, 0:E], upb[:], picked[s.par(RL)][:], start=True, stop=True)
                pe.matmul(ml[:, E:2 * E], onesb[:], picked[s.par(RL)][:], start=True, stop=True).then_inc(ml_written, 1)

            def slot(s):
                def run(lag, f, *args):
                    if s.on(lag):
                        f(s, *args)
                run(5, max_scores, "C", 0)
                run(5, max_scores, "C", 1)
                run(4, project, "C")
                run(3, out_proj, "S")
                run(5, max_scores, "C", 2)
                run(7, turn_norm, "C")
                run(5, max_scores, "C", 3)
                run(6, weigh, "C")
                run(5, turn_max, "C")
                run(0, project, "S")
                run(7, logits)
                run(2, exp_scores, "S", 0)
                run(2, exp_scores, "S", 1)
                run(1, max_scores, "S", 0)
                run(2, exp_scores, "S", 2)
                run(1, max_scores, "S", 1)
                run(2, exp_scores, "S", 3)
                run(3, turn_norm, "S")
                run(1, max_scores, "S", 2)
                run(6, out_proj, "C")
                run(1, max_scores, "S", 3)
                run(5, values, "C")
                run(1, values, "S")
                run(2, weigh, "S")
                run(5, exp_scores, "C", 0)
                run(5, exp_scores, "C", 1)
                run(1, turn_max, "S")
                run(-1, turn, "trx")
                run(5, exp_scores, "C", 2)
                run(7, prefix)
                run(5, exp_scores, "C", 3)
                run(3, turn, "trc")
            each_slot(pe, slot)

            pe.wait_ge(mq_read, MQ.total())
            pe.wait_ge(ml_read, ML.total())
            pe.wait_ge(od_read, OD.total())
            pe.wait_ge(s1_read, S1.total())
            pe.wait_ge(s2_read, S2.total())
            pe.wait_ge(plan_dve, NPLAN)
            pe.wait_ge(ld_w, 16)
            pe.wait_ge(b_moved, 16)

            def tile_slot(s):
                i = s.i
                at = i if s.t is None else s.value(i, 1)

                if s.on(1):
                    e = pe.value_load(tile_e[0:1, bass.ds(at - 1, 1)], min_val=0, max_val=E - 1)
                if s.on(0):
                    wait(pe, x_read, s, i + 1, 1)
                    wait(pe, w1_in[i % RING], s, 16 * (i // RING + 1), 16 // RING)
                    wait(pe, h_read, s, i - 1, 1)
                    for c in range(FC):
                        mm = pe.matmul(psH[i % 2][:, c * P:c * P + P], w1g[i % RING][:, c * P:c * P + P], xgT[i % 2][:],
                                       start=True, stop=True)
                    mm.then_inc(h_written, 1)
                if s.on(-2):
                    j = i + 2
                    wait(pe, xg_in[j % RING], s, 16 * (j // RING + 1), 16 // RING)
                    wait(pe, x_read, s, j - 1, 1)
                    pe.transpose(psX[j % 2][:, 0:P], xg[j % RING][:, 0:D], ident).then_inc(x_written, 1)
                if s.on(1):
                    j = i - 1
                    wait(pe, h_read, s, j + 1, 1)
                    wait(pe, y_done, s, j - 1, 1)
                    pe.matmul(psY[j % 2][:, 0:D], onesb[0:3, :],
                              bp[:].rearrange("k e f -> k (e f)")[:, bass.ds(e * D, D)], start=True, stop=False)
                    for c in range(FC):
                        mm = pe.matmul(psY[j % 2][:, 0:D], hT[j % 2][:, c * P:c * P + P],
                                       w2t[:].rearrange("p e c d -> p (e c d)")[:, bass.ds(e * FC * D + c * D, D)],
                                       start=False, stop=(c == FC - 1))
                    mm.then_inc(y_written, 1)
            each_tile(pe, tile_slot)

        @block.scalar
        def _(act):
            def exps(s, a, j):
                wait(act, s2_written, s, S2.before(s, a) + j + 1, S2.rate)
                if s.i - LAG2[a] > 0:
                    wait(act, av_done, s, OD.before(Slot(s.i - 1 - LAG2[a] + WEIGH[a]), a) + 1, OD.rate)
                act.activation(pT[a][j][:], ps2[j % 2][:].rearrange("p (h q) -> p h q", h=HG), ACT.Exp,
                               scale=SCALE).then_inc(s2_read, 1)

            def projected(s, a):
                k, b, p = s.par(PROJ[a]), s.i - PROJ[a], pre[a]
                wait(act, mq_written, s, MQ.before(s, "proj" + a) + 1, MQ.rate)
                if b >= 2:
                    wait(act, left[a], s, 2 * b - 2, 2)
                act.activation(qk[a][k][:, 0, :], mq[:, 0:P], ACT.Identity, bias=cb[p + "bk"])
                act.activation(qk[a][k][:, 1, :], mq[:, P:2 * P], ACT.Identity, bias=cb[p + "bq"]).then_inc(mq_read, 1)

            def part(s, a, n):
                b, k = s.i - PROJ[a], s.par(PROJ[a])
                if n == 0:
                    wait(act, mq_read, s, MQ.before(s, "proj" + a) + 1, MQ.rate)
                    if b >= 2:
                        wait(act, parts_out[a][k], s, 16 * (b // 2), 8)
                else:
                    wait(act, left[a], s, 2 * b + 1, 2)
                act.activation(parts[a][k][:, :, n, :], (qk if n == 0 else remain)[a][k][:], ACT.Copy)\
                    .then_inc(cast[a], 1)

            def affine(s, a):
                k, p = s.par(ROWL[a]), {"S": "ln1_", "C": "ln2_"}[a]
                wait(act, mq_written, s, MQ.before(s, "zt" + a) + 1, MQ.rate)
                act.activation((x1T if a == "S" else x2T)[k][:], mq[:, 0:P], ACT.Identity, scale=cb[p + "g"],
                               bias=cb[p + "b"]).then_inc(mq_read, 1)

            def valued(s, a):
                wait(act, mq_written, s, MQ.before(s, "v" + a) + 1, MQ.rate)
                k, b = s.par(VAL[a]), s.i - VAL[a]
                if b >= 2:
                    wait(act, av_done, s, OD.before(Slot(s.i - 2 - VAL[a] + WEIGH[a]), a) + 1, OD.rate)
                act.activation(v[a][k][:], mq[:, 0:D], ACT.Copy).then_inc(mq_read, 1)

            def move(s, kind, dst):
                wait(act, mq_written, s, MQ.before(s, kind) + 1, MQ.rate)
                if kind[:2] == "mt":
                    b = s.i - TURN1[kind[2]]
                    if b >= 2:
                        wait(act, row_in[kind[2]][b % 2], s, 16 * (b // 2), 8)
                act.activation(dst, mtb if kind[:2] == "mt" else mq[:, 0:P], ACT.Copy).then_inc(mq_read, 1)

            act.wait_ge(ld_const, 16 * NLOAD)

            def router_exp(s):
                k = s.par(RL)
                wait(act, rt_dve, s, RT * (s.i - RL) + 2, RT)
                act.activation(ex[k][:], lg[k][:], ACT.Exp, bias=neg[k][:], accum_out=esum[k][:]).then_inc(rt_act, 1)

            def router_two(s):
                k = s.par(RL)
                wait(act, rt_dve, s, RT * (s.i - RL) + 5, RT)
                act.activation(e2[k][:], pmax[k][:, 0:1], ACT.Exp, scale=-1.0, bias=pmax[k][:, 1:2]).then_inc(rt_act, 1)

            def slot(s):
                def run(lag, f, *args):
                    if s.on(lag):
                        f(s, *args)
                run(4, projected, "C")
                run(7, affine, "C")
                run(4, part, "C", 0)
                run(4, part, "C", 1)
                run(5, move, "mtC", nmaxT["C"][s.par(5)][:])
                run(0, projected, "S")
                run(2, exps, "S", 0)
                run(0, part, "S", 0)
                run(2, exps, "S", 1)
                run(7, router_exp)
                run(0, part, "S", 1)
                run(2, exps, "S", 2)
                run(2, exps, "S", 3)
                run(3, affine, "S")
                run(7, router_two)
                run(5, valued, "C")
                run(1, valued, "S")
                run(5, exps, "C", 0)
                run(1, move, "mtS", nmaxT["S"][s.par(1)][:])
                run(5, exps, "C", 1)
                run(-1, move, "trx", xT[s.par(-1)][:])
                run(5, exps, "C", 2)
                run(3, move, "trc", cT[s.par(3)][:])
                run(5, exps, "C", 3)
            each_slot(act, slot)
            act.wait_ge(blank_set, 3)
            pad(act, range(E // 2, E))

            def tile_slot(s):
                i = s.i
                if s.on(0):
                    wait(act, h_written, s, i + 1, 1)
                    if i >= 2:
                        wait(act, y_written, s, i - 1, 1)
                    for c in range(FC):
                        ins = act.activation(hT[i % 2][:, c * P:c * P + P], psH[i % 2][:, c * P:c * P + P], ACT.Gelu,
                                             bias=w1g[i % RING][:, FF + c:FF + c + 1])
                    ins.then_inc(h_read, 1)
                if s.on(-2):
                    j = i + 2
                    wait(act, x_written, s, j + 1, 1)
                    if j >= 2:
                        wait(act, h_written, s, j - 1, 1)
                    act.activation(xgT[j % 2][:], psX[j % 2][:, 0:P], ACT.Copy).then_inc(x_read, 1)
            each_tile(act, tile_slot)

            for q in range(NQ):
                k = q % NF
                act.wait_ge(fin_shift, q + 1)
                for c in range(4):
                    ins = act.activation(yout[k][:, c, :], yout[k][:, c, :], ACT.Identity, bias=fshift[k][:, c:c + 1],
                                         scale=frstd[k][:, c:c + 1])
                ins.then_inc(fin_z, 1)

        @block.vector
        def _(dve):
            for a in AB:
                for k in range(2):
                    for st in stack[a][k]:
                        dve.memset(st[:], 0.0).then_inc(stack_zero, 1)
            for k in range(2):
                dve.memset(R[k][:, :, D + 3:D + 4], 0.0)
                dve.memset(R[k][:, 0, D + 1:D + 2], 1.0)
                dve.memset(R[k][:, 1, D + 1:D + 2], 0.0).then_inc(R_set, 1)
            dve.wait_ge(ld_const, 16 * NLOAD)
            dve.tensor_scalar(base[:], cst[:, C_I8:C_I8 + E], float(REGION), None, ALU.mult).then_inc(base_set, 1)
            dve.tensor_copy(dstf[:], cst[:, C_DST:C_DST + 2]).then_inc(base_set, 1)
            dve.wait_ge(base_set, 2)
            dve.wait_ge(ld_rows, 16 * NROWS)
            dve.wait_ge(radd_mm, 1)
            for k, a in enumerate(AB):
                dve.tensor_tensor(radd[a][:], ml[:, k * D:k * D + D], rr[pre[a] + "bo"], ALU.add).then_inc(radd_done, 1)
            dve.wait_ge(radd_done, 2)
            dve.tensor_tensor(radd["C"][:], radd["C"][:], rr["ln1_b"], ALU.add).then_inc(radd_done, 1)

            def split_biases():
                dve.wait_ge(ld_b, 16)
                rest = bt
                for k in range(3):
                    dve.tensor_copy(bpart[k][:], rest[:]).then_inc(b_split, 1)
                    dve.wait_ge(b_split, 2 * k + 1)
                    if k < 2:
                        dve.tensor_tensor(brest[k][:], rest[:], bpart[k][:], ALU.subtract).then_inc(b_split, 1)
                        dve.wait_ge(b_split, 2 * k + 2)
                        rest = brest[k]

            def maxima(s, a, j):
                wait(dve, s1_written, s, S1.before(s, a) + j + 1, S1.rate)
                if j == 0 and s.i - LAG1[a] >= 2:
                    wait(dve, mq_written, s, MQ.before(Slot(s.i - 2), "mt" + a) + 1, MQ.rate)
                dve.tensor_reduce(nmax[a][s.par(LAG1[a])][:, HG * j:HG * j + HG],
                                  ps1[j % 2][:].rearrange("p (h k) -> p h k", h=HG), AX.X, ALU.max,
                                  negate=True).then_inc(s1_read, 1)

            def less(s, a, part):
                k, b = s.par(PROJ[a]), s.i - PROJ[a]
                wait(dve, cast[a], s, 2 * b + part + 1, 2)
                if part == 1:
                    wait(dve, left[a], s, 2 * b + 1, 2)
                dve.tensor_tensor(remain[a][k][:] if part == 0 else parts[a][k][:, :, 2, :],
                                  (qk if part == 0 else remain)[a][k][:], parts[a][k][:, :, part, :],
                                  ALU.subtract).then_inc(left[a], 1)

            def normalise_sum(s, a):
                wait(dve, av_done, s, OD.before(s, a) + 1, OD.rate)
                dve.reciprocal(rden[:], pd[:, 0:P]).then_inc(rden_done, 1)

            def normalise(s, a):
                n = OD.before(s, a)
                wait(dve, rden_done, s, n + 1, OD.rate)
                if s.i - WEIGH[a] >= 1:
                    wait(dve, ml_written, s, ML.before(Slot(s.i - 1 - WEIGH[a] + END[a]), "wo" + a) + 1, ML.rate)
                dve.tensor_tensor(oT[a][:], po[:].rearrange("p (h q) -> p h q", h=HG),
                                  rden[:].rearrange("p (o q) -> p o q", o=1).broadcast_to([P, HG, P]),
                                  ALU.mult).then_inc(od_read, 1)

            def residual(s, a):
                b, k = s.i - END[a], s.par(END[a])
                n = ML.before(s, "wo" + a)
                wait(dve, ml_written, s, n + 1, ML.rate)
                wait(dve, xb_done[a], s, b + 1, 1)
                dve.tensor_tensor(res[a][k][:], ml[:, 0:D], xb[a][k][:], ALU.add).then_inc(ml_read, 1)

            def normal(s, a):
                b, k = s.i - END[a], s.par(END[a])
                wait(dve, ln_pool[a], s, 2 * b + 2, 2)
                wait(dve, ln_dve[a], s, 4 * b + 3, 4)
                dve.tensor_scalar(z[a][k][:], res[a][k][:], mv[a][k][:, 0:1], rstd[a][k][:],
                                  ALU.subtract, ALU.mult).then_inc(ln_dve[a], 1)

            def chain(s, lag, n):
                wait(dve, rt_dve, s, RT * (s.i - lag) + n, RT)

            def router(s, step):
                k, b = s.par(RL), s.i - RL
                if step == "logits":
                    wait(dve, ml_written, s, ML.before(s, "log") + 1, ML.rate)
                    dve.tensor_tensor(lg[k][:], ml[:, 0:E], rbt[:], ALU.add).then_inc(ml_read, 1)
                elif step == "maximum":
                    wait(dve, ml_read, s, ML.before(s, "log") + 1, ML.rate)
                    dve.tensor_reduce(neg[k][:], lg[k][:], AX.X, ALU.max, negate=True).then_inc(rt_dve, 2)
                elif step == "over sum":
                    wait(dve, rt_act, s, 2 * b + 1, 2)
                    dve.reciprocal(rsum[k][:], esum[k][:]).then_inc(rt_dve, 1)
                elif step == "probabilities":
                    chain(s, RL, 3)
                    dve.tensor_scalar(prob[k][:], ex[k][:], rsum[k][:], None, ALU.mult).then_inc(rt_dve, 1)
                elif step == "largest":
                    chain(s, RL, 4)
                    dve.tensor_tensor(ride[:], neg[k][:], neg[k][:], ALU.add)
                    dve.max(pmax[k][:], prob[k][:]).then_inc(rt_dve, 1)
                elif step == "whose":
                    chain(s, RL, 5)
                    dve.tensor_tensor(ride[:], neg[k][:], neg[k][:], ALU.add)
                    dve.max_index(pidx[k][:], pmax[k][:], prob[k][:]).then_inc(rt_dve, 1)
                elif step == "whose, float32":
                    chain(s, RL, 6)
                    dve.tensor_copy(pidf[k][:], pidx[k][:, 0:2]).then_inc(rt_dve, 1)
                elif step == "one-hot":
                    chain(s, RL, 7)
                    dve.tensor_tensor(hot[k][:], cst[:, C_I8:C_I8 + E].rearrange("p (o e) -> p o e", o=1)
                                      .broadcast_to([P, 2, E]),
                                      pidf[k][:].rearrange("p (c o) -> p c o", o=1).broadcast_to([P, 2, E]),
                                      ALU.is_equal).then_inc(rt_dve, 1)
                elif step == "picked":
                    chain(s, RL, 8)
                    dve.tensor_tensor(picked[k][:], hot[k][:, 0, :], hot[k][:, 1, :], ALU.add).then_inc(rt_dve, 1)
                elif step == "sum of two":
                    if b >= 2:
                        wait(dve, scattered[k], s, 32 * (b // 2), 16)
                    wait(dve, rt_act, s, 2 * b + 2, 2)
                    dve.tensor_scalar(wden[k][:], e2[k][:], 1.0, None, ALU.add).then_inc(rt_dve, 1)
                elif step == "first weight":
                    chain(s, RL, 10)
                    dve.reciprocal(R[k][:, 0, D:D + 1], wden[k][:]).then_inc(rt_dve, 1)
                elif step == "second weight":
                    chain(s, RL, 11)
                    dve.tensor_tensor(R[k][:, 1, D:D + 1], R[k][:, 0, D:D + 1], e2[k][:], ALU.mult).then_inc(rt_dve, 1)
                    dve.tensor_copy(R[k][:, :, D + 2:D + 3].bitcast(U32),
                                    dstf[:].rearrange("p (c o) -> p c o", o=1)).then_inc(rt_dve, 1)
                elif step == "target rows":
                    chain(s, RL, 13)
                    dve.tensor_scalar(dstf[:], dstf[:], float(2 * P), None, ALU.add).then_inc(rt_dve, 1)
                elif step == "place":
                    wait(dve, ml_written, s, ML.before(s, "pre") + 1, ML.rate)
                    dve.tensor_tensor(place[k][:], ml[:, 0:E], base[:], ALU.add).then_inc(rt_dve, 1)
                elif step == "new base":
                    chain(s, RL, 15)
                    dve.tensor_tensor(base[:], ml[:, E:2 * E], base[:], ALU.add).then_inc(ml_read, 1)
                    dve.tensor_tensor(hotp[k][:], hot[k][:], place[k][:].rearrange("p (o e) -> p o e", o=1)
                                      .broadcast_to([P, 2, E]), ALU.mult).then_inc(rt_dve, 1)
                elif step == "row":
                    chain(s, RL, 16)
                    dve.tensor_reduce(rowf[k][:], hotp[k][:], AX.X, ALU.add).then_inc(rt_dve, 1)
                elif step == "row, integer":
                    chain(s, RL, 17)
                    dve.tensor_copy(rown[k][:], rowf[k][:]).then_inc(rt_dve, 1)

            def residual_stats(s, a):
                b, k = s.i - END[a], s.par(END[a])
                wait(dve, ml_read, s, ML.before(s, "wo" + a) + 1, ML.rate)
                dve.bn_stats(stat[a][k][:], res[a][k][:]).then_inc(ln_dve[a], 1)

            def residual_aggr(s, a):
                b, k = s.i - END[a], s.par(END[a])
                wait(dve, ln_dve[a], s, 4 * b + 1, 4)
                dve.bn_aggr(mv[a][k][:], stat[a][k][:]).then_inc(ln_dve[a], 2)

            def slot(s):
                def run(lag, f, *args):
                    if s.on(lag):
                        f(s, *args)
                if s.t is None and s.i == 2:
                    split_biases()
                run(5, maxima, "C", 0)
                run(5, maxima, "C", 1)
                run(5, maxima, "C", 2)
                run(3, residual, "S")
                run(4, less, "C", 0)
                run(5, maxima, "C", 3)
                run(3, residual_stats, "S")
                run(4, less, "C", 1)
                run(3, residual_aggr, "S")
                run(6, normalise_sum, "C")
                run(7, router, "logits")
                run(6, normalise, "C")
                run(7, router, "maximum")
                run(3, normal, "S")
                run(0, less, "S", 0)
                run(1, maxima, "S", 0)
                run(7, router, "over sum")
                run(7, router, "probabilities")
                run(0, less, "S", 1)
                run(1, maxima, "S", 1)
                run(7, router, "largest")
                run(6, residual, "C")
                run(7, router, "whose")
                run(7, router, "whose, float32")
                run(6, residual_stats, "C")
                run(7, router, "one-hot")
                run(7, router, "picked")
                run(1, maxima, "S", 2)
                run(6, residual_aggr, "C")
                run(6, normal, "C")
                run(1, maxima, "S", 3)
                run(7, router, "sum of two")
                run(2, normalise_sum, "S")
                run(7, router, "first weight")
                run(7, router, "second weight")
                run(2, normalise, "S")
                run(7, router, "target rows")
                run(7, router, "place")
                run(7, router, "new base")
                run(7, router, "row")
                run(7, router, "row, integer")
            each_slot(dve, slot)
            dve.wait_ge(rt_dve, RT * B)
            plan_tiles(dve)

            def tile_slot(s):
                if s.on(1):
                    i = s.i - 1
                    wait(dve, y_written, s, i + 1, 1)
                    wait(dve, xf_done, s, i + 1, 1)
                    if i >= RING:
                        wait(dve, y_sent[i % RING], s, 16 * (i // RING), 16 // RING)
                    dve.scalar_tensor_tensor(out=ysb[i % RING][:], in0=psY[i % 2][:, 0:D], scalar=xg[i % RING][:, D:D + 1],
                                             in1=xf[i % RING][:], op0=ALU.mult, op1=ALU.add).then_inc(y_done, 1)
            each_tile(dve, tile_slot)

            def sum_and_stats(q):
                k = q % NF
                dve.wait_ge(y_back[k], 16 * (q // NF + 1))
                if q >= NF:
                    dve.wait_ge(stored[k], 16 * (q // NF))
                dve.tensor_tensor(yout[k][:], yin[k][:, :, 0, :], yin[k][:, :, 1, :], ALU.add).then_inc(fin_dve, 1)
                dve.wait_ge(fin_dve, 3 * q + 1)
                for c in range(4):
                    ins = dve.bn_stats(fstat[k][:, c, :], yout[k][:, c, :])
                ins.then_inc(fin_dve, 1)
                dve.wait_ge(fin_dve, 3 * q + 2)
                for c in range(4):
                    ins = dve.bn_aggr(fmv[k][:, c, :], fstat[k][:, c, :])
                ins.then_inc(fin_dve, 1)

            for q in range(NQ + 2):
                if q < NQ:
                    sum_and_stats(q)
                if 1 <= q <= NQ:
                    k = (q - 1) % NF
                    dve.wait_ge(fin_rstd, 2 * q)
                    dve.scalar_tensor_tensor(out=fshift[k][:], in0=fmv[k][:, :, 0], scalar=-1.0, in1=frstd[k][:],
                                             op0=ALU.mult, op1=ALU.mult).then_inc(fin_shift, 1)
                if q >= 2:
                    k = (q - 2) % NF
                    dve.wait_ge(fin_z, q - 1)
                    dve.tensor_tensor(yout[k][:], yout[k][:], row4("ln3_g"), ALU.mult).then_inc(fin_g, 1)

        @block.gpsimd
        def _(pool):
            pool.memset(nhalf[:], -0.5).then_inc(cast_done, 1)
            pool.memset(eps[:], EPS).then_inc(cast_done, 1)
            pool.wait_ge(ld_const, 16 * NLOAD)
            for dst, c, w in ((identb[:], C_ID, P), (upb[:], C_UP, P), (onesb[:], C_ONE, P),
                              (negmask[:].rearrange("p h q -> p (h q)"), C_CM, HG * P)):
                pool.tensor_copy(dst, cst[:, c:c + w]).then_inc(cast_done, 1)
            for h in range(HG):
                for a in AB:
                    pool.tensor_tensor(wom[a][:, h, :], W[pre[a] + "wo"], cst[:, C_HM + h:C_HM + h + 1].broadcast_to([P, D]),
                                       ALU.mult).then_inc(cast_done, 1)
                pool.wait_ge(cast_done, 6 + 4 * h + 2)
                pool.memset(onem[:, h, :], 0.0).then_inc(cast_done, 1)
                pool.wait_ge(cast_done, 6 + 4 * h + 3)
                pool.memset(onem[:, h, h * HD:h * HD + HD], 1.0).then_inc(cast_done, 1)
            pool.wait_ge(cast_done, NCAST)
            pool.wait_ge(radd_done, 3)
            pool.wait_ge(ld_rows, 16 * NROWS)
            pool.memset(blank[:], 0.0).then_inc(blank_set, 1)
            pool.iota(blank_dst[:], pattern=[[P, NE]], base=2 * TOK, channel_multiplier=1).then_inc(blank_set, 1)
            pool.wait_ge(blank_set, 2)
            pool.tensor_copy(blank[:, :, D + 2:D + 3].bitcast(U32), blank_dst[:].rearrange("p (n o) -> p n o", o=1))\
                .then_inc(blank_set, 1)

            def causal(s, j):
                wait(pool, sel_done, s, G * (s.i - 2) + j, G)
                wait(pool, s2_read, s, S2.before(s, "S") + j + 1, S2.rate)
                pool.tensor_tensor(carrier[:], nhalf[:], nhalf[:], ALU.mult)
                pool.affine_select(out=pT["S"][j][:], in_=pT["S"][j][:], compare_op=ALU.is_ge, fill=0.0, base=0,
                                   pattern=[[0, HG], [1, P]], channel_multiplier=-1).then_inc(sel_done, 1)

            def inv_std(s, a):
                b, k = s.i - END[a], s.par(END[a])
                wait(pool, ln_dve[a], s, 4 * b + 3, 4)
                pool.tensor_tensor(ve[a][k][:], mv[a][k][:, 1:2], eps[:], ALU.add).then_inc(ln_pool[a], 1)
                wait(pool, ln_pool[a], s, 2 * b + 1, 2)
                pool.tensor_tensor(rstd[a][k][:], ve[a][k][:], nhalf[:], ALU.pow).then_inc(ln_pool[a], 1)

            def rows_out(s, a):
                b, k = s.i - ROWL[a], s.par(ROWL[a])
                wait(pool, ln_dve[a], s, 4 * b + 4, 4)
                if a == "S" and b >= 2:
                    wait(pool, xb_done["C"], s, b - 1, 1)
                g = rr["ln1_g" if a == "S" else "ln2_g"]
                pool.tensor_tensor(zg[a][k][:], z[a][k][:], g, ALU.mult).then_inc(row_pool[a], 1)
                if a == "C":
                    wait(pool, row_pool[a], s, 3 * b + 1, 3)
                    if b >= 2:
                        wait(pool, scattered[k], s, 32 * (b // 2), 16)
                    for c in range(2):
                        pool.tensor_tensor(R[k][:, c, 0:D], zg[a][k][:], rr["ln2_b"], ALU.add).then_inc(row_pool[a], 1)

            def base_rows(s, a):
                lag = 2 if a == "S" else 5
                b, k = s.i - lag, s.par(lag)
                if a == "S":
                    wait(pool, ld_r[k], s, 16 * (b // 2 + 1), 8)
                else:
                    wait(pool, row_pool["S"], s, b + 1, 1)
                if b >= 2:
                    wait(pool, ln_dve[a], s, 4 * (b - 2) + 1, 4)
                pool.tensor_tensor(xb[a][k][:], xr[k][:] if a == "S" else zg["S"][k][:], radd[a][:], ALU.add)\
                    .then_inc(xb_done[a], 1)

            def scatter(s):
                k = s.par(SL)
                wait(pool, rode, s, s.i - SL, 1)
                wait(pool, row_pool["C"], s, 3 * (s.i - SL) + 3, 3)
                wait(pool, rt_dve, s, RT * (s.i - SL) + 18, RT)
                pool.tensor_tensor(ride_pool[:], nhalf[:], nhalf[:], ALU.mult).then_inc(rode, 1)
                for c in range(2):
                    pool.indirect_dma_start(out=xs, out_offset=bass.IndirectOffsetOnAxis(ap=rown[k][:, c:c + 1], axis=0),
                                            in_=R[k][:, c, :], in_offset=None).then_inc(scattered[k], 16)

            def slot(s):
                def run(lag, f, *args):
                    if s.on(lag):
                        f(s, *args)
                run(8, scatter)
                run(3, inv_std, "S")
                run(5, base_rows, "C")
                run(2, causal, 0)
                run(2, causal, 1)
                run(3, rows_out, "S")
                run(2, causal, 2)
                run(2, causal, 3)
                run(2, base_rows, "S")
                run(6, inv_std, "C")
                run(7, rows_out, "C")
            each_slot(pool, slot)

            def tile_slot(s):
                if s.on(1):
                    wait(pool, y_done, s, s.i, 1)
                if s.on(0):
                    i = s.i
                    wait(pool, xg_in[i % RING], s, 16 * (i // RING + 1), 16 // RING)
                    if i >= RING:
                        wait(pool, y_done, s, i - RING + 1, 1)
                    pool.tensor_tensor(xf[i % RING][:], xg[i % RING][:, 0:D], xg[i % RING][:, D + 1:D + 2].broadcast_to([P, D]),
                                       ALU.mult).then_inc(xf_done, 1)
                if s.on(1):
                    i = s.i - 1
                    pool.indirect_dma_start(out=ys, out_offset=bass.IndirectOffsetOnAxis(
                        ap=xg[i % RING][:, D + 2:D + 3].bitcast(U32), axis=0), in_=ysb[i % RING][:, :], in_offset=None)\
                        .then_inc(y_sent[i % RING], 16)
            each_tile(pool, tile_slot)

            for q in range(NQ + 2):
                if q < NQ:
                    k = q % NF
                    pool.wait_ge(fin_dve, 3 * q + 3)
                    pool.tensor_tensor(fve[k][:], fmv[k][:, :, 1], eps[:].broadcast_to([P, 4]), ALU.add).then_inc(fin_rstd, 1)
                    pool.wait_ge(fin_rstd, 2 * q + 1)
                    pool.tensor_tensor(frstd[k][:], fve[k][:], nhalf[:].broadcast_to([P, 4]), ALU.pow).then_inc(fin_rstd, 1)
                if q >= 2:
                    k = (q - 2) % NF
                    pool.wait_ge(fin_g, q - 1)
                    pool.tensor_tensor(yout[k][:], yout[k][:], row4("ln3_b"), ALU.add).then_inc(fin_pool, 1)


NCAST, NPLAN = 6 + 4 * HG, 14


def constants():
    import numpy as np
    c = np.zeros((P, NCONST), np.float32)
    p = np.arange(P)
    c[:, C_ID:C_ID + P] = np.eye(P)
    for h in range(HG):
        c[:, C_CM + h * P:C_CM + h * P + P] = np.where(p[None, :] > p[:, None], -1e30, 0.0)
    c[:, C_UP:C_UP + P] = p[:, None] < p[None, :]
    c[:, C_ONE:C_ONE + P] = 1.0
    c[:, C_I8:C_I8 + E] = np.arange(E)
    c[:, C_DST:C_DST + 2] = 2 * p[:, None] + np.arange(2)
    c[:, C_I72:C_I72 + TILES] = np.arange(TILES)
    c[:, C_HM:C_HM + HG] = p[:, None] // HD % HG == np.arange(HG)
    return c


def kernel(**inputs):
    import numpy as np
    import concourse.bacc as bacc
    from concourse.bass_utils import run_bass_kernel_spmd as run

    def arr(name):
        a = np.asarray(inputs["L0_xattn_" + name])
        if name[-2:] in ("wq", "wk", "bq", "bk"):
            a = a.reshape(a.shape[:-1] + (H, HD)).swapaxes(-1, -2).reshape(a.shape)
        return np.ascontiguousarray(a)

    arrays = {
        "x": np.ascontiguousarray(inputs["x"]), "ctx_in": np.ascontiguousarray(inputs["ctx_1024"]),
        "const": constants(), "cols": np.ascontiguousarray(np.stack([arr(n) for n in COLS], 1)),
        "rows": np.stack([arr(n) for n in ROWS]), "mats": np.stack([arr(n) for n in MATS]),
        "rw": arr("router_w"), "rb": arr("router_b"), 
        "w1": np.concatenate([arr("e_w1"), arr("e_b1").reshape(E, FC, P).swapaxes(1, 2)], axis=2),
        "w2": arr("e_w2"), "b2": arr("e_b2"),
    }
    nc = bacc.Bacc("TRN2", target_bir_lowering=False, num_devices=1)
    aps = {n: nc.dram_tensor(n, a.shape, mybir.dt.from_np(a.dtype), kind="ExternalInput").ap() for n, a in arrays.items()}
    out = nc.dram_tensor("out", (B, P, D), F32, kind="ExternalOutput").ap()
    build(nc, out=out, **aps)
    got = run(nc, [arrays], core_ids=[0])
    return got.results[0]["out"]
```
